# Optimizing a Trainium2 kernel written in Bass

```python
import numpy as np
import jax
import jax.numpy as jnp

def _softmax(x, axis=-1):
    return jax.nn.softmax(x, axis=axis)

def _gelu(x):
    return jax.nn.gelu(x, approximate=True)

def _silu(x):
    return jax.nn.silu(x)

def _sigmoid(x):
    return jax.nn.sigmoid(x)

def _layernorm(x, axis=-1, eps=1e-05):
    m = jnp.mean(x, axis=axis, keepdims=True)
    v = jnp.var(x, axis=axis, keepdims=True)
    return (x - m) / jnp.sqrt(v + eps)

def _scatter_add(tgt, idx, src, axis=0):
    return tgt.at[idx].add(src)

def _segment_sum(src, seg, n):
    return jax.ops.segment_sum(src, seg, n)
kernel_name = 'mk_adj_ffn_d1_adj_r2_3ca6a2'

def setup_inputs(seed: int=0):
    np.random.seed(seed)
    _w = jnp.asarray

    def _rec_inputs():
        import jax
        import jax.numpy as jnp
        _gk = jax.random.key(seed)
        x = -0.0002928 + 1 * jax.random.normal(jax.random.fold_in(_gk, 1), (128, 128, 128), jnp.float32)
        _a = jax.random.bernoulli(jax.random.fold_in(_gk, 2), 0.125, (128, 128))
        adj = _a.astype(jnp.int32)
        return (x, adj)
    x, adj = _rec_inputs()

    def _L0_gnn_setup():
        import jax, jax.numpy as jnp
        import numpy as np
        LEAKY_ALPHA = 0.2
        key = jax.random.key(seed)
        k1, k2, k3, k4 = jax.random.split(key, 4)
        B, N, Fin, Fout = (8, 1024, 128, 128)
        h = jax.random.normal(k1, (B, N, Fin), dtype=jnp.float32)
        adj = jax.random.randint(k2, (N, N), 0, 2, dtype=jnp.int32)
        W = jax.random.normal(k3, (Fin, Fout), dtype=jnp.float32) * (1.414 * (6.0 / (Fin + Fout)) ** 0.5)
        a = jax.random.normal(k4, (2 * Fout, 1), dtype=jnp.float32) * (1.414 * (6.0 / (2 * Fout + 1)) ** 0.5)
        return {'h': h, 'adj': adj, 'W': W, 'a': a}
    _L0_gnn_all = _L0_gnn_setup()
    _L0_gnn_in = {k: v for k, v in _L0_gnn_all.items() if k in ('W', 'a')}
    del _L0_gnn_all

    def _L0_ffn_setup():
        import jax, jax.numpy as jnp
        import numpy as np
        TOP_K = 2
        LN_EPS = 1e-05
        key = jax.random.key(seed)
        ks = jax.random.split(key, 8)
        B, S, D, E, H = (16, 512, 128, 8, 512)
        x = jax.random.normal(ks[0], (B, S, D), dtype=jnp.float32)
        Wr = jax.random.normal(ks[1], (D, E), dtype=jnp.float32) * 0.1
        br = jnp.zeros((E,), dtype=jnp.float32)
        ln_g = jnp.ones((E, D), dtype=jnp.float32)
        ln_b = jnp.zeros((E, D), dtype=jnp.float32)
        W1 = jax.random.normal(ks[2], (E, D, H), dtype=jnp.float32) * (1.0 / np.sqrt(D))
        b1 = jnp.zeros((E, H), dtype=jnp.float32)
        W2 = jax.random.normal(ks[3], (E, H, D), dtype=jnp.float32) * (1.0 / np.sqrt(H))
        b2 = jnp.zeros((E, D), dtype=jnp.float32)
        return {'x': x, 'Wr': Wr, 'br': br, 'ln_g': ln_g, 'ln_b': ln_b, 'W1': W1, 'b1': b1, 'W2': W2, 'b2': b2}
    _L0_ffn_all = _L0_ffn_setup()
    _L0_ffn_in = {k: v for k, v in _L0_ffn_all.items() if k in ('Wr', 'br', 'ln_g', 'ln_b', 'W1', 'b1', 'W2', 'b2')}
    del _L0_ffn_all
    return {'x': x, 'adj': adj, 'L0_gnn_W': _L0_gnn_in['W'], 'L0_gnn_a': _L0_gnn_in['a'], 'L0_ffn_Wr': _L0_ffn_in['Wr'], 'L0_ffn_br': _L0_ffn_in['br'], 'L0_ffn_ln_g': _L0_ffn_in['ln_g'], 'L0_ffn_ln_b': _L0_ffn_in['ln_b'], 'L0_ffn_W1': _L0_ffn_in['W1'], 'L0_ffn_b1': _L0_ffn_in['b1'], 'L0_ffn_W2': _L0_ffn_in['W2'], 'L0_ffn_b2': _L0_ffn_in['b2']}

def reference(x, adj, L0_gnn_W, L0_gnn_a, L0_ffn_Wr, L0_ffn_br, L0_ffn_ln_g, L0_ffn_ln_b, L0_ffn_W1, L0_ffn_b1, L0_ffn_W2, L0_ffn_b2):
    import jax
    import jax.numpy as jnp

    def _L0_gnn_ref(h, adj, W, a):
        import jax, jax.numpy as jnp
        import numpy as np
        LEAKY_ALPHA = 0.2
        Fout = W.shape[1]
        Wh = jnp.einsum('bnf,fo->bno', h, W)
        a1 = a[:Fout, 0]
        a2 = a[Fout:, 0]
        s_i = Wh @ a1
        s_j = Wh @ a2
        e = jax.nn.leaky_relu(s_i[:, :, None] + s_j[:, None, :], negative_slope=LEAKY_ALPHA)
        N = Wh.shape[1]
        mask = (adj > 0) | jnp.eye(N, dtype=bool)
        e = jnp.where(mask[None, :, :], e, -jnp.inf)
        attention = jax.nn.softmax(e, axis=-1)
        attention = jnp.nan_to_num(attention, nan=0.0)
        h_prime = jnp.einsum('bij,bjo->bio', attention, Wh)
        return jax.nn.elu(h_prime)

    def _L0_ffn_ref(x, Wr, br, ln_g, ln_b, W1, b1, W2, b2):
        import jax, jax.numpy as jnp
        import numpy as np
        TOP_K = 2
        LN_EPS = 1e-05
        B, S, D = x.shape
        N = B * S
        xt = x.reshape(N, D)
        logits = xt @ Wr + br
        probs = jax.nn.softmax(logits, axis=-1)
        top_p, top_idx = jax.lax.top_k(probs, TOP_K)
        weights = top_p / top_p.sum(axis=-1, keepdims=True)
        mu = xt.mean(axis=-1, keepdims=True)
        var = ((xt - mu) ** 2).mean(axis=-1, keepdims=True)
        xn = (xt - mu) * jax.lax.rsqrt(var + LN_EPS)
        xe = xn[None, :, :] * ln_g[:, None, :] + ln_b[:, None, :]
        h = jax.nn.gelu(jnp.einsum('end,edh->enh', xe, W1) + b1[:, None, :], approximate=False)
        y = jnp.einsum('enh,ehd->end', h, W2) + b2[:, None, :]
        y_tok = jnp.transpose(y, (1, 0, 2))
        sel = jnp.take_along_axis(y_tok, top_idx[:, :, None], axis=1)
        out = (weights[:, :, None] * sel).sum(axis=1)
        return out.reshape(B, S, D)
    x = x + _L0_gnn_ref(_layernorm(x, axis=-1), adj, L0_gnn_W, L0_gnn_a)
    x = x + _L0_ffn_ref(_layernorm(x, axis=-1), L0_ffn_Wr, L0_ffn_br, L0_ffn_ln_g, L0_ffn_ln_b, L0_ffn_W1, L0_ffn_b1, L0_ffn_W2, L0_ffn_b2)
    return x

_drawn_inputs = setup_inputs


def setup_inputs(seed=0):
    import zlib

    import numpy as np

    out = dict(_drawn_inputs(seed))
    spreads = {'L0_ffn_br': (0.0, 0.1),
     'L0_ffn_ln_g': (1.0, 0.2),
     'L0_ffn_ln_b': (0.0, 0.286),
     'L0_ffn_b1': (0.0, 0.288),
     'L0_ffn_b2': (0.0, 0.1)}
    factors = {}
    for name, (base, spread) in spreads.items():
        noise = np.random.default_rng([zlib.crc32(name.encode()), seed]).standard_normal(out[name].shape)
        drawn = base * np.exp(spread * noise) if base else spread * noise
        out[name] = jnp.asarray(drawn.astype(out[name].dtype))
    for name, factor in factors.items():
        out[name] = (out[name] * factor).astype(out[name].dtype)
    return out
```

```python
import concourse.bass as bass
from concourse import mybir
from contextlib import ExitStack

F32 = mybir.dt.float32
F16 = mybir.dt.float16
BF16 = mybir.dt.bfloat16
I32 = mybir.dt.int32
ALU = mybir.AluOpType
ACT = mybir.ActivationFunctionType
AXX = mybir.AxisListType.X

B, N, D = 128, 128, 128
E, H = 8, 512
HC = H // 128
GB = 4
NG = B // GB
CB = 8
BLK = 4 * GB
PAIRS = 2 * B * N
TP = 256
NT = PAIRS // TP + E
RB, YB = 8, 4
CAP = B * N + TP
ROW = D + 2
EPS = 1e-5
ROUTE = 19
SLOPE = 0.2
NEG = -1e30
WS = 64.0


def program(nc, x, adj, W, a, Wr, br, ln_g, ln_b, W1, b1, W2, b2, out):
    ctx = ExitStack()
    with ctx:
        def sb(name, shape, dt=F32):
            return ctx.enter_context(nc.sbuf_tensor(name, shape, dt))

        def sem(name):
            return ctx.enter_context(nc.semaphore(name))

        rows_d = nc.dram_tensor("rows_d", [E * CAP + TP, ROW], I32).ap()
        y_d = nc.dram_tensor("y_d", [PAIRS, D], F32).ap()

        ps = ctx.enter_context(nc.psum_tensor("ps", [128, 8, 512], F32))

        def bank(n):
            return ps[:, n, :].rearrange("p (b d) -> p b d", b=GB)
        ps_hT, ps_wh, ps_s, ps_pT, ps_att, ps_xT = (bank(n) for n in range(6))
        ps_l = ps[:, 6, 0:GB * E].rearrange("p (b e) -> p b e", e=E)
        ps_r = ps[:, 7, 0:BLK * E].rearrange("p (b e) -> p b e", e=E)

        ident = sb("ident", [128, 128])
        ident16 = sb("ident16", [128, 128], F16)
        ones_b = sb("ones_b", [128, 128], BF16)
        tri_b = sb("tri_b", [128, 128], BF16)
        ones2 = sb("ones2", [2, 128], F16)
        minus_half = sb("minus_half", [128, 2 * GB])
        rev = sb("rev", [128, E])
        ecap = sb("ecap", [128, E])
        ids = sb("ids", [128, B, 2], I32)
        pad = sb("pad", [128, ROW], I32)
        tile_no = sb("tile_no", [1, NT])
        iota_i = sb("iota_i", [128, 2 * E + NT], I32)
        zero8 = sb("zero8", [1, E])
        adj_i = sb("adj_i", [128, 128], I32)
        mask_bias = sb("mask_bias", [128, 128])
        w_gnn = sb("w_gnn", [128, 128])
        w_gnnT = sb("w_gnnT", [128, 128])
        small_rows = sb("small_rows", [64, 128])
        cols = sb("cols", [128, 64])
        wa = sb("wa", [128, 2])
        wa1_rep = sb("wa1_rep", [128, 128])
        wa2_rep = sb("wa2_rep", [128, 128])
        wr = sb("wr", [128, E])
        br_row = sb("br_row", [1, E])
        br_rep = sb("br_rep", [128, E])
        ones_row = sb("ones_row", [1, 128])
        g_ws = sb("g_ws", [128, E])
        w_stage = sb("w_stage", [128, 2, H])
        w1h = sb("w1h", [128, E * H], F16)
        w1l = sb("w1l", [128, E * H], F16)
        w2h = sb("w2h", [128, E * H], F16)
        w2l = sb("w2l", [128, E * H], F16)
        b1c = sb("b1c", [128, E * HC])
        b2_f = sb("b2_f", [1, E * D])
        b2_h = sb("b2_h", [1, E * D], F16)
        b2_l = sb("b2_l", [1, E * D], F16)
        b2_hl = sb("b2_hl", [2, E * D], F16)
        x1 = sb("x1", [128, B, D])
        xhl = sb("xhl", [128, 4, GB, 2 * D], F16)
        st1 = sb("st1", [128, 2, GB, 6])
        mv1 = sb("mv1", [128, 2, GB, 2])
        veps1 = sb("veps1", [128, 2, GB])
        rstd1 = sb("rstd1", [128, 2, GB])
        h = sb("h", [128, 2, GB, D])
        hT = sb("hT", [128, 2, GB, 128])
        wh = sb("wh", [128, 2, GB, D])
        e_sc = sb("e_sc", [128, 2, GB, 128])
        p = sb("p", [128, 2, GB, 128])
        nmx = sb("nmx", [128, 2, GB])
        sm = sb("sm", [128, 2, GB])
        rsm = sb("rsm", [128, 2, GB])
        pT = sb("pT", [128, 2, GB, 128])
        hp = sb("hp", [128, 2, GB, D])
        mn = sb("mn", [128, 2, GB, D])
        st2 = sb("st2", [128, 2, GB, 6])
        mv2 = sb("mv2", [128, 2, GB, 2])
        vq = sb("vq", [128, 2, 2 * GB])
        rec2 = sb("rec2", [128, 2, GB])
        rq = sb("rq", [128, 2, 2 * GB])
        rtot = sb("rtot", [128, 2, GB])
        unsc = sb("unsc", [128, 2, GB])
        xn = sb("xn", [128, 2, GB, D])
        xnT = sb("xnT", [128, 2, GB, 128])
        lg = sb("lg", [128, BLK, E])
        lg2 = sb("lg2", [128, BLK, E])
        eq = sb("eq", [128, BLK, E])
        top1 = sb("top1", [128, BLK])
        top2 = sb("top2", [128, BLK])
        pick = sb("pick", [128, 2, BLK])
        oh1 = sb("oh1", [128, BLK, E])
        oh2 = sb("oh2", [128, BLK, E])
        both = sb("both", [128, BLK, E], BF16)
        blk_sum = sb("blk_sum", [128, E])
        seen = sb("seen", [128, E])
        seen_b = sb("seen_b", [128, E], BF16)
        gap = sb("gap", [128, BLK])
        egap = sb("egap", [128, BLK])
        den = sb("den", [128, BLK])
        rk = sb("rk", [128, BLK, E])
        pos = sb("pos", [128, 2, BLK])
        meta = sb("meta", [128, 2, BLK, 2], I32)
        row_out = sb("row_out", [128, 2, 2, GB, ROW], I32)
        idx = sb("idx", [128, 2, 2 * GB], I32)
        til_i = sb("til_i", [1, E], I32)
        til = sb("til", [1, E])
        t0 = sb("t0", [1, E + 1])
        jump = sb("jump", [1, E])
        past = sb("past", [1, NT])
        rf = sb("rf", [1, NT])
        ef = sb("ef", [1, NT])
        tabs = sb("tabs", [1, 2 * NT + E], I32)
        row_in = sb("row_in", [128, RB, 2, ROW], I32)
        rT = sb("rT", [128, 2, 2 * TP], F16)
        yw = sb("yw", [128, YB, 2, D])

        s_const = sem("s_const")
        s_w_rows = sem("s_w_rows")
        s_cols_T = sem("s_cols_T")
        s_cols = sem("s_cols")
        s_wT_T = sem("s_wT_T")
        s_wT = sem("s_wT")
        s_wa_mm = sem("s_wa_mm")
        s_wa = sem("s_wa")
        s_reps = sem("s_reps")
        s_prep = sem("s_prep")
        s_w_staged = sem("s_w_staged")
        s_w_hi = sem("s_w_hi")
        s_w_lo = sem("s_w_lo")
        s_b1_mm = sem("s_b1_mm")
        s_b1c = sem("s_b1c")
        s_b2_parts = sem("s_b2_parts")
        s_b2_moved = sem("s_b2_moved")
        s_x_in = sem("s_x_in")
        s_stats1 = sem("s_stats1")
        s_aggr1 = sem("s_aggr1")
        s_veps1 = sem("s_veps1")
        s_rstd1 = sem("s_rstd1")
        s_h = sem("s_h")
        s_hT_ps = sem("s_hT_ps")
        s_hT = sem("s_hT")
        s_wh_ps = sem("s_wh_ps")
        s_wh = sem("s_wh")
        s_s_ps = sem("s_s_ps")
        s_e = sem("s_e")
        s_leaky = sem("s_leaky")
        s_nmx = sem("s_nmx")
        s_p = sem("s_p")
        s_pT_ps = sem("s_pT_ps")
        s_pT = sem("s_pT")
        s_att_ps = sem("s_att_ps")
        s_rsm = sem("s_rsm")
        s_hp = sem("s_hp")
        s_mn = sem("s_mn")
        s_ex = sem("s_ex")
        s_elu = sem("s_elu")
        s_x1 = sem("s_x1")
        s_stats2 = sem("s_stats2")
        s_aggr2 = sem("s_aggr2")
        s_vq_chain = sem("s_vq_chain")
        s_vq = sem("s_vq")
        s_rq = sem("s_rq")
        s_scales = sem("s_scales")
        s_xn = sem("s_xn")
        s_xn_hi = sem("s_xn_hi")
        s_xn_lo = sem("s_xn_lo")
        s_xT_ps = sem("s_xT_ps")
        s_xT = sem("s_xT")
        s_l_ps = sem("s_l_ps")
        s_l = sem("s_l")
        s_route = sem("s_route")
        s_gap = sem("s_gap")
        s_egap = sem("s_egap")
        s_both = sem("s_both")
        s_seen = sem("s_seen")
        s_rank_ps = sem("s_rank_ps")
        s_rows1 = sem("s_rows1")
        s_rows2 = sem("s_rows2")
        s_cnt_ps = sem("s_cnt_ps")
        s_tab_chain = sem("s_tab_chain")
        s_tab = sem("s_tab")
        s_pads = sem("s_pads")
        s_rT_ps = sem("s_rT_ps")
        s_rT = sem("s_rT")
        s_up_ps = sem("s_up_ps")
        s_gelu = sem("s_gelu")
        s_hid_hi = sem("s_hid_hi")
        s_hid_lo = sem("s_hid_lo")
        s_down_ps = sem("s_down_ps")
        s_yw = sem("s_yw")
        s_c_half = sem("s_c_half")
        s_c_sum = sem("s_c_sum")
        s_stored = sem("s_stored")
        s_scat = [sem(f"s_scat{n}") for n in range(2)]
        s_rows_in = [sem(f"s_rows_in{n}") for n in range(RB)]
        s_y_out = [sem(f"s_y_out{n}") for n in range(YB)]
        s_y_in = [sem(f"s_y_in{n}") for n in range(2)]

        def since(n, first):
            return not isinstance(n, int) or n >= first

        class Chain:
            def __init__(self, eng, sem, base, steps):
                self.eng, self.sem, self.base, self.steps, self.n = eng, sem, base, steps, 0

            def __call__(self, ins):
                self.n += 1
                ins.then_inc(self.sem, 1)
                self.eng.wait_ge(self.sem, self.base + self.n)

            def end(self):
                assert self.n == self.steps, self.n

        def group(g):
            return not isinstance(g, int) or 0 <= g < NG

        def of(g, b=None):
            return bass.ds(g * GB, GB) if b is None else bass.ds(g * GB + b, 1)

        def x1_of(g, b):
            return x1[:, of(g, b), :].rearrange("p a d -> p (a d)")

        LOOP_A = 9
        TURNS_A = (NG - 3 - LOOP_A) // 4

        def phase_a(eng, slot):
            for s in range(-3, LOOP_A):
                slot(s, s % 4, (s - 5) // 4)
            with eng.Fori(0, TURNS_A) as i:
                for k in range(4):
                    slot(i * 4 + (LOOP_A + k), (LOOP_A + k) % 4, i + (LOOP_A - 5) // 4)
            for s in range(LOOP_A + 4 * TURNS_A, NG + 5):
                slot(s, s % 4, (s - 5) // 4)

        def routes(s, k):
            return k == 1 and not (isinstance(s, int) and s < 5)

        TURNS_B = (NT - 2 - 2) // RB

        def phase_b(eng, slot):
            for s in range(-2, 2):
                slot(s, s % RB)
            with eng.Fori(0, TURNS_B) as i:
                for k in range(RB):
                    slot(i * RB + (2 + k), (2 + k) % RB)
            for s in range(2 + RB * TURNS_B, NT):
                slot(s, s % RB)

        def tile(t):
            return not isinstance(t, int) or 0 <= t < NT

        def ps_rT(q):
            return ps[:, q, 0:TP].bitcast(F16)

        def ps_up(q):
            return ps[:, 2 + 2 * q:4 + 2 * q, :].rearrange("p b (c t) -> p (b c) t", t=TP)

        def ps_y(q):
            return ps[:, 6 + q, 0:TP].rearrange("p (s d) -> p s d", s=2)

        def hid(q):
            return (e_sc, p)[q][:, :, :, :].rearrange("p a b n -> p (a b n)").rearrange("p (c t) -> p c t", c=HC)

        def part_of(buf, q):
            return buf[:, q, :, :].rearrange("p b n -> p (b n)").bitcast(F16).rearrange("p (c t) -> p c t", c=HC)

        def hid_h(q):
            return part_of(h, q)

        def hid_l(q):
            return part_of(xn, q)


        def y_in(q):
            return (w1h, w1l)[q][:, :].bitcast(F32).rearrange("p (b d) -> p b d", b=CB)

        block = ctx.enter_context(nc.Block())

        @block.sync
        def _(sp):
            xv = x.rearrange("b n d -> n b d")

            def load_x(i):
                if since(i, 1):
                    sp.wait_ge(s_x_in, i * 16)
                v = bass.ds(i * CB, CB)
                sp.dma_start(x1[:, v, :], xv[:, v, :]).then_inc(s_x_in, 16)

            load_x(0)
            load_x(1)
            for dst, src in [(adj_i[:, :], adj), (w_gnn[:, :], W), (wr[:, :], Wr),
                             (br_row[:, :], br.rearrange("(o e) -> o e", o=1)),
                             (small_rows[0:32, :], b1.rearrange("e (c p) -> (e c) p", p=128)),
                             (small_rows[32:40, :], ln_g), (small_rows[40:48, :], ln_b),
                             (small_rows[48:50, :], a.rearrange("(r p) o -> r (p o)", r=2)),
                             (b2_f[:, :], b2.rearrange("(o e) d -> o (e d)", o=1))]:
                sp.dma_start(dst, src).then_inc(s_w_rows, 16)
            for n in range(2 * E):
                if n >= 1:
                    sp.wait_ge(s_w_staged, 16 * n)
                if n >= 2:
                    sp.wait_ge(s_w_lo, n - 1)
                if n >= 2 and n % 2 == 0:
                    sp.wait_ge(s_b1_mm, n // 2)
                if n % 2 == 0:
                    src, dst = W1[n // 2], w_stage[:, 0, :]
                else:
                    src = W2[n // 2].rearrange("(c p) d -> p c d", p=128)
                    dst = w_stage[:, 1, :].rearrange("p (c d) -> p c d", c=HC)
                sp.dma_start(dst, src).then_inc(s_w_staged, 16)
                if n in (5, 9):
                    load_x(2 if n == 5 else 3)
            sp.wait_ge(s_b2_parts, 2)
            sp.dma_start(b2_hl[0:1, :], b2_h[:, :]).then_inc(s_b2_moved, 16)
            sp.dma_start(b2_hl[1:2, :], b2_l[:, :]).then_inc(s_b2_moved, 16)
            with sp.Fori(4, B // CB) as i:
                load_x(i)

            sp.wait_ge(s_tab, 1)
            for q in range(2):
                sp.wait_ge(s_scat[q], 128 * (NG // 2))
            no_pair = pad[:, :].rearrange("p (c r) -> p c r", c=1).to_broadcast([128, TP // 128, ROW])
            for e in range(E):
                n_e = sp.value_load(tabs[0:1, 2 * NT + e:2 * NT + e + 1], min_val=0, max_val=B * N)
                sp.dma_start(rows_d[bass.ds(n_e + e * CAP, TP), :].rearrange("(c p) r -> p c r", p=128),
                             no_pair).then_inc(s_pads, 16)
            sp.dma_start(rows_d[E * CAP:E * CAP + TP, :].rearrange("(c p) r -> p c r", p=128),
                         no_pair).then_inc(s_pads, 16)
            sp.wait_ge(s_pads, 16 * (E + 1))

            def load_rows(t, k):
                r = sp.value_load(tabs[0:1, bass.ds(t, 1)], min_val=0, max_val=E * CAP)
                sp.dma_start(row_in[:, k, :, :], rows_d[bass.ds(r, TP), :].rearrange("(c p) r -> p c r", p=128))\
                    .then_inc(s_rows_in[k], 16)

            for k in range(RB):
                load_rows(k, k)
            with sp.Fori(1, NT // RB) as i:
                for k in range(RB):
                    sp.wait_ge(s_rT_ps, i * RB + (k - RB + 1))
                    sp.wait_ge(s_yw, i * RB + (k - RB + 1))
                    sp.wait_ge(s_y_out[k % YB], i * (32 * RB // YB) + (k // YB - 1) * 32)
                    load_rows(i * RB + k, k)

            for q in range(YB):
                sp.wait_ge(s_y_out[q], 32 * NT // YB)
            yv = y_d.rearrange("(b n k) d -> n b (k d)", n=N, k=2)
            ov = out.rearrange("b n d -> n b d")

            def load_y(c, q):
                sp.dma_start(y_in(q), yv[:, bass.ds(c * CB, CB), :]).then_inc(s_y_in[q], 16)

            def store(c):
                sp.wait_ge(s_c_sum, c + 1)
                v = bass.ds(c * CB, CB)
                sp.dma_start(ov[:, v, :], x1[:, v, :]).then_inc(s_stored, 16)

            for q in range(2):
                load_y(q, q)
            with sp.Fori(0, B // CB // 2 - 1) as i:
                for q in range(2):
                    store(i * 2 + q)
                    load_y(i * 2 + (2 + q), q)
            for q in range(2):
                store(B // CB - 2 + q)
            sp.wait_ge(s_stored, 16 * (B // CB))

        @block.gpsimd
        def _(pool):
            for t, v in ((ident, 0.0), (tri_b, 1.0), (ones_b, 1.0), (ones2, 1.0), (ones_row, 1.0),
                         (minus_half, -0.5), (seen, 0.0), (zero8, 0.0)):
                pool.memset(t[:, :], v).then_inc(s_const, 1)
            pool.memset(pad[:, 0:D], 0).then_inc(s_const, 1)
            pool.memset(pad[:, D:D + 1], PAIRS).then_inc(s_const, 1)
            pool.memset(pad[:, D + 1:ROW], 0).then_inc(s_const, 1)
            pool.iota(ids[:, :, :], pattern=[[2 * N, B], [1, 2]], base=0, channel_multiplier=2).then_inc(s_const, 1)
            pool.iota(iota_i[:, 0:E], pattern=[[-1, E]], base=E, channel_multiplier=0).then_inc(s_const, 1)
            pool.iota(iota_i[:, E:2 * E], pattern=[[CAP, E]], base=0, channel_multiplier=0).then_inc(s_const, 1)
            pool.iota(iota_i[:, 2 * E:], pattern=[[1, NT]], base=0, channel_multiplier=0).then_inc(s_const, 1)
            pool.wait_ge(s_const, 15)
            pool.affine_select(out=ident[:, :], in_=ident[:, :], compare_op=ALU.not_equal, fill=1.0, base=0,
                               pattern=[[-1, 128]], channel_multiplier=1).then_inc(s_const, 1)
            pool.affine_select(out=tri_b[:, :], in_=tri_b[:, :], compare_op=ALU.is_gt, fill=0.0, base=0,
                               pattern=[[1, 128]], channel_multiplier=-1).then_inc(s_const, 1)

            def slot(s, k, j):
                g, q = s + 3, (k + 3) % 2
                if group(g):
                    pool.wait_ge(s_const, 17)
                    pool.wait_ge(s_veps1, g + 1)
                    pool.tensor_tensor(rstd1[:, q, :], veps1[:, q, :], minus_half[:, 0:GB], ALU.pow).then_inc(s_rstd1, 1)
                g, q = s, k % 2
                if group(g):
                    pool.wait_ge(s_vq, g + 1)
                    pool.tensor_tensor(rq[:, q, :], vq[:, q, :], minus_half[:, :], ALU.pow).then_inc(s_rq, 1)
                g, q = s - 5, (k - 5) % 2
                if group(g):
                    pool.wait_ge(s_rows1, g + 1)
                    pool.wait_ge(s_rows2, g + 1)
                    pool.nop(nofuse=True)
                    for n in range(2 * GB):
                        pool.indirect_dma_start(
                            rows_d[:, :], bass.IndirectOffsetOnAxis(ap=idx[:, q, n:n + 1], axis=0),
                            row_out[:, q, n // GB, n % GB, :], None).then_inc(s_scat[q], 16)
            phase_a(pool, slot)

            def slot_b(s, k):
                if tile(s) and not (isinstance(s, int) and s < 0):
                    pool.wait_ge(s_yw, s + 1)
                    pool.nop(nofuse=True)
                    for c in range(2):
                        pool.indirect_dma_start(
                            y_d[:, :],
                            bass.IndirectOffsetOnAxis(ap=row_in[:, k, c, D:D + 1], axis=0),
                            yw[:, k % YB, c, :], None, bounds_check=PAIRS - 1,
                            oob_is_err=False).then_inc(s_y_out[k % YB], 16)
            phase_b(pool, slot_b)

        @block.scalar
        def _(act):
            def slot(s, k, j):
                if isinstance(s, int) and s + 3 < E:
                    e = s + 3
                    act.wait_ge(s_cols, 2)
                    act.wait_ge(s_w_staged, 16 * (2 * e + 1))
                    act.activation(w1h[:, e * H:(e + 1) * H], w_stage[:, 0, :], ACT.Copy,
                                   scale=g_ws[:, e:e + 1]).then_inc(s_w_hi, 1)
                    act.wait_ge(s_w_staged, 16 * (2 * e + 2))
                    act.activation(w2h[:, e * H:(e + 1) * H], w_stage[:, 1, :], ACT.Copy, scale=WS).then_inc(s_w_hi, 1)
                g, q = s + 1, (k + 1) % 2
                if group(g):
                    act.wait_ge(s_nmx, g + 1)
                    for b in range(GB):
                        last = act.activation(p[:, q, b, :], p[:, q, b, :], ACT.Exp, bias=nmx[:, q, b:b + 1],
                                              accum_out=sm[:, q, b:b + 1])
                    last.then_inc(s_p, 1)
                g, q = s, k % 2
                if group(g):
                    act.wait_ge(s_mn, g + 1)
                    act.activation(mn[:, q, :, :], mn[:, q, :, :], ACT.Exp).then_inc(s_ex, 1)
                g, q = s + 2, k % 2
                if group(g):
                    act.wait_ge(s_hT_ps, g + 1)
                    if since(g, 2):
                        act.wait_ge(s_s_ps, g - 1)
                    act.copy(hT[:, q, :, :], ps_hT).then_inc(s_hT, 1)
                g, q = s + 1, (k + 1) % 2
                if group(g):
                    act.wait_ge(s_pT_ps, g + 1)
                    if since(g, 2):
                        act.wait_ge(s_att_ps, g - 1)
                    act.copy(pT[:, q, :, :], ps_pT).then_inc(s_pT, 1)
                g, q = s + 2, k % 2
                if group(g):
                    act.wait_ge(s_wh_ps, g + 1)
                    if since(g, 2):
                        act.wait_ge(s_att_ps, g - 1)
                    act.copy(wh[:, q, :, :], ps_wh).then_inc(s_wh, 1)
                if routes(s, k):
                    act.wait_ge(s_gap, j + 1)
                    act.activation(egap[:, :], gap[:, :], ACT.Exp).then_inc(s_egap, 1)
                g, q = s - 5, (k - 5) % 2
                if group(g):
                    if since(g, 2):
                        act.wait_ge(s_scat[q], (g - q) * 64)
                    act.wait_ge(s_rows1, g + 1)
                    act.copy(row_out[:, q, 1, :, 0:D].bitcast(F16), row_out[:, q, 0, :, 0:D].bitcast(F16)).then_inc(s_rows2, 1)
                g, q = s - 1, (k - 1) % 2
                if group(g):
                    act.wait_ge(s_xT_ps, g + 1)
                    if since(g, 2):
                        act.wait_ge(s_l_ps, g - 1)
                    act.copy(xnT[:, q, :, :], ps_xT).then_inc(s_xT, 1)
            phase_a(act, slot)
            act.wait_ge(s_tab, 1)

            def slot_b(s, k):
                t, q = s + 2, k % 2
                if tile(t):
                    act.wait_ge(s_rT_ps, t + 1)
                    if since(t, 2):
                        act.wait_ge(s_up_ps, t - 1)
                    act.copy(rT[:, q, :], ps_rT(q)).then_inc(s_rT, 1)
                t, q = s + 1, (k + 1) % 2
                if tile(t):
                    e = act.value_load(tabs[0:1, bass.ds(t + NT, 1)], min_val=0, max_val=E - 1)
                    act.wait_ge(s_up_ps, t + 1)
                    if since(t, 2):
                        act.wait_ge(s_hid_lo, t - 1)
                    for c in range(HC):
                        last = act.activation(hid(q)[:, c, :], ps_up(q)[:, c, :], ACT.Gelu,
                                              bias=b1c[:, bass.ds(e * HC + c, 1)], scale=1.0 / WS)
                    last.then_inc(s_gelu, 1)
                t, q = s, k % 2
                if tile(t):
                    act.wait_ge(s_down_ps, t + 1)
                    r = k % YB
                    if since(t, YB):
                        act.wait_ge(s_y_out[r], (t - r) * (32 // YB))
                    for c in range(2):
                        last = act.activation(yw[:, r, c, :], ps_y(q)[:, c, :], ACT.Copy,
                                              scale=row_in[:, k, c, D + 1:ROW].bitcast(F32))
                    last.then_inc(s_yw, 1)
            phase_b(act, slot_b)

        @block.vector
        def _(dve):
            def spread(ap, shape, dim):
                return ap.unsqueeze(dim).to_broadcast(shape)

            dve.wait_ge(s_const, 17)
            dve.tensor_copy(ident16[:, :], ident[:, :])
            dve.tensor_copy(rev[:, :], iota_i[:, 0:E])
            dve.tensor_copy(ecap[:, :], iota_i[:, E:2 * E])
            dve.tensor_copy(tile_no[:, :], iota_i[0:1, 2 * E:]).then_inc(s_prep, 1)
            dve.wait_ge(s_w_rows, 16 * 9)
            prep = Chain(dve, s_prep, 1, 3)
            prep(dve.tensor_scalar(mask_bias[:, :], adj_i[:, :], 0.0, None, ALU.is_gt))
            prep(dve.tensor_tensor(mask_bias[:, :], mask_bias[:, :], ident[:, :], ALU.max))
            prep(dve.tensor_scalar(mask_bias[:, :], mask_bias[:, :], 1.0, -NEG, ALU.subtract, ALU.mult))
            prep.end()
            dve.tensor_scalar(b2_h[:, :], b2_f[:, :], WS, None, ALU.mult).then_inc(s_b2_parts, 1)
            dve.wait_ge(s_b2_parts, 1)
            dve.scalar_tensor_tensor(b2_l[:, :], b2_f[:, :], WS, b2_h[:, :], ALU.mult, ALU.subtract).then_inc(s_b2_parts, 1)
            dve.wait_ge(s_cols_T, 1)
            dve.tensor_copy(cols[:, 0:50], ps[:, 0, 0:50]).then_inc(s_cols, 1)
            dve.wait_ge(s_cols, 1)
            dve.tensor_scalar(g_ws[:, :], cols[:, 32:40], WS, None, ALU.mult).then_inc(s_cols, 1)
            dve.wait_ge(s_wT_T, 1)
            dve.tensor_copy(w_gnnT[:, :], ps[:, 1, 0:128]).then_inc(s_wT, 1)
            dve.wait_ge(s_wa_mm, 1)
            dve.tensor_copy(br_rep[:, :], ps[:, 2, 2:2 + E])
            dve.tensor_copy(wa[:, :], ps[:, 2, 0:2]).then_inc(s_wa, 1)
            dve.wait_ge(s_wa, 1)
            dve.tensor_copy(wa1_rep[:, :], wa[:, 0:1].to_broadcast([128, 128]))
            dve.tensor_copy(wa2_rep[:, :], wa[:, 1:2].to_broadcast([128, 128])).then_inc(s_reps, 1)

            def norm_stats(g, q, st, mv, stats, aggr):
                dve.nop(nofuse=True)
                for b in range(GB):
                    last = dve.bn_stats(st[:, q, b, :], x1_of(g, b))
                last.then_inc(stats, 1)
                dve.wait_ge(stats, g + 1)
                dve.nop(nofuse=True)
                for b in range(GB):
                    last = dve.bn_aggr(mv[:, q, b, :], st[:, q, b, :])
                last.then_inc(aggr, 1)
                dve.wait_ge(aggr, g + 1)

            def scores(g, q):
                dve.wait_ge(s_s_ps, g + 1)
                dve.tensor_tensor(e_sc[:, q, :, :], ps_s, spread(mask_bias[:, :], [128, GB, 128], 1), ALU.add).then_inc(s_e, 1)
                dve.wait_ge(s_e, g + 1)
                if since(g, 2):
                    dve.wait_ge(s_pT_ps, g - 1)
                dve.scalar_tensor_tensor(p[:, q, :, :], e_sc[:, q, :, :], SLOPE, e_sc[:, q, :, :],
                                         ALU.mult, ALU.max).then_inc(s_leaky, 1)
                dve.wait_ge(s_leaky, g + 1)
                dve.tensor_reduce(nmx[:, q, :], p[:, q, :, :], AXX, ALU.max, negate=True).then_inc(s_nmx, 1)

            def attended(g, q):
                dve.wait_ge(s_p, g + 1)
                dve.reciprocal(rsm[:, q, :], sm[:, q, :]).then_inc(s_rsm, 1)
                dve.wait_ge(s_rsm, g + 1)
                dve.wait_ge(s_att_ps, g + 1)
                dve.tensor_tensor(hp[:, q, :, :], ps_att, spread(rsm[:, q, :], [128, GB, D], 2), ALU.mult).then_inc(s_hp, 1)
                dve.wait_ge(s_hp, g + 1)
                dve.tensor_scalar(mn[:, q, :, :], hp[:, q, :, :], 0.0, None, ALU.min).then_inc(s_mn, 1)

            def first_norm(g, q):
                dve.wait_ge(s_rstd1, g + 1)
                if since(g, 2):
                    dve.wait_ge(s_hT_ps, g - 1)
                for b in range(GB):
                    last = dve.tensor_scalar(h[:, q, b, :], x1_of(g, b), mv1[:, q, b, 0:1], rstd1[:, q, b:b + 1],
                                             ALU.subtract, ALU.mult)
                last.then_inc(s_h, 1)

            def first_stats(g, q, k):
                dve.wait_ge(s_x_in, (g - k % 2) * 8 + 16)
                norm_stats(g, q, st1, mv1, s_stats1, s_aggr1)
                dve.tensor_scalar(veps1[:, q, :], mv1[:, q, :, 1], EPS, None, ALU.add).then_inc(s_veps1, 1)

            def residual(g, q):
                dve.wait_ge(s_ex, g + 1)
                dve.scalar_tensor_tensor(hp[:, q, :, :], hp[:, q, :, :], 0.0, mn[:, q, :, :], ALU.max, ALU.add).then_inc(s_elu, 1)
                dve.wait_ge(s_elu, g + 1)
                dve.scalar_tensor_tensor(x1[:, of(g), :], hp[:, q, :, :], -1.0, x1[:, of(g), :], ALU.add, ALU.add).then_inc(s_x1, 1)
                dve.wait_ge(s_x1, g + 1)
                norm_stats(g, q, st2, mv2, s_stats2, s_aggr2)
                c = Chain(dve, s_vq_chain, g * 3, 3)
                c(dve.tensor_scalar(vq[:, q, 0:GB], mv2[:, q, :, 1], EPS, None, ALU.add))
                c(dve.reciprocal(rec2[:, q, :], vq[:, q, 0:GB]))
                c(dve.tensor_tensor(vq[:, q, GB:], rec2[:, q, :], mv2[:, q, :, 1], ALU.mult))
                c.end()
                dve.tensor_scalar(vq[:, q, GB:], vq[:, q, GB:], EPS, None, ALU.add).then_inc(s_vq, 1)

            def logits(g, q, k):
                dve.wait_ge(s_l_ps, g + 1)
                dve.tensor_tensor(lg[:, k * GB:(k + 1) * GB, :], ps_l, spread(unsc[:, q, :], [128, GB, E], 2),
                                  ALU.mult).then_inc(s_l, 1)

            def tokens(g, q, k):
                dve.wait_ge(s_rq, g + 1)
                dve.tensor_tensor(unsc[:, q, :], vq[:, q, GB:], rq[:, q, GB:], ALU.mult)
                dve.tensor_tensor(rtot[:, q, :], rq[:, q, 0:GB], rq[:, q, GB:], ALU.mult).then_inc(s_scales, 1)
                dve.wait_ge(s_scales, g + 1)
                if since(g, 2):
                    dve.wait_ge(s_xT_ps, g - 1)
                for b in range(GB):
                    last = dve.tensor_scalar(xn[:, q, b, :], x1_of(g, b), mv2[:, q, b, 0:1], rtot[:, q, b:b + 1],
                                             ALU.subtract, ALU.mult)
                last.then_inc(s_xn, 1)
                dve.wait_ge(s_xn, g + 1)
                dve.tensor_copy(xhl[:, k, :, 0:D], xn[:, q, :, :]).then_inc(s_xn_hi, 1)
                dve.wait_ge(s_xn_hi, g + 1)
                dve.tensor_tensor(xhl[:, k, :, D:2 * D], xn[:, q, :, :], xhl[:, k, :, 0:D], ALU.subtract).then_inc(s_xn_lo, 1)

            ALLE = [128, BLK, E]

            def picks(j, c):
                dve.wait_ge(s_l, j * 4 + 4)
                c(dve.tensor_tensor(lg[:, :, :], lg[:, :, :], spread(br_rep[:, :], ALLE, 1), ALU.add))
                for src, top, oh, n in ((lg, top1, oh1, 0), (lg2, top2, oh2, 1)):
                    c(dve.tensor_reduce(top[:, :], src[:, :, :], AXX, ALU.max))
                    c(dve.tensor_tensor(eq[:, :, :], src[:, :, :], spread(top[:, :], ALLE, 2), ALU.is_equal))
                    c(dve.tensor_tensor(eq[:, :, :], eq[:, :, :], spread(rev[:, :], ALLE, 1), ALU.mult))
                    c(dve.tensor_reduce(pick[:, n, :], eq[:, :, :], AXX, ALU.max))
                    c(dve.tensor_tensor(oh[:, :, :], spread(pick[:, n, :], ALLE, 2), spread(rev[:, :], ALLE, 1),
                                        ALU.is_equal))
                    if n == 0:
                        c(dve.scalar_tensor_tensor(lg2[:, :, :], oh1[:, :, :], -3e38, lg[:, :, :], ALU.mult, ALU.add))
                        dve.tensor_copy(seen_b[:, :], seen[:, :]).then_inc(s_seen, 1)
                dve.tensor_tensor(both[:, :, :], oh1[:, :, :], oh2[:, :, :], ALU.add).then_inc(s_both, 1)
                dve.tensor_tensor(gap[:, :], top2[:, :], top1[:, :], ALU.subtract).then_inc(s_gap, 1)

            def places(j, c, k, ids_of):
                dve.wait_ge(s_both, j + 1)
                c(dve.tensor_reduce(blk_sum[:, :], both[:, :, :].rearrange("p b e -> p e b"), AXX, ALU.add))
                dve.tensor_tensor(seen[:, :], seen[:, :], blk_sum[:, :], ALU.add)
                dve.wait_ge(s_egap, j + 1)
                c(dve.tensor_scalar(den[:, :], egap[:, :], 1.0, None, ALU.add))
                c(dve.reciprocal(den[:, :], den[:, :]))
                c(dve.tensor_scalar(meta[:, 0, :, 1].bitcast(F32), den[:, :], 1.0 / WS, None, ALU.mult))
                dve.tensor_tensor(meta[:, 1, :, 1].bitcast(F32), meta[:, 0, :, 1].bitcast(F32), egap[:, :], ALU.mult)
                for n in range(2):
                    dve.tensor_copy(meta[:, n, :, 0], ids[:, ids_of, n])
                dve.wait_ge(s_rank_ps, j + 1)
                c(dve.tensor_tensor(rk[:, :, :], ps_r, spread(ecap[:, :], ALLE, 1), ALU.add))
                dve.tensor_tensor(eq[:, :, :], rk[:, :, :], oh1[:, :, :], ALU.mult)
                c(dve.tensor_tensor(lg2[:, :, :], rk[:, :, :], oh2[:, :, :], ALU.mult))
                dve.tensor_reduce(pos[:, 0, :], eq[:, :, :], AXX, ALU.add)
                c(dve.tensor_reduce(pos[:, 1, :], lg2[:, :, :], AXX, ALU.add))

            def rows(g, q, k):
                if since(g, 2):
                    dve.wait_ge(s_scat[q], (g - q) * 64)
                dve.wait_ge(s_xn_lo, g + 1)
                dve.tensor_copy(row_out[:, q, 0, :, 0:D].bitcast(F16), xhl[:, k, :, :])
                for n in range(2):
                    dve.tensor_copy(row_out[:, q, n, :, D:ROW], meta[:, n, k * GB:(k + 1) * GB, :])
                dve.tensor_copy(idx[:, q, :].rearrange("p (n b) -> p n b", n=2),
                                pos[:, :, k * GB:(k + 1) * GB]).then_inc(s_rows1, 1)

            def slot(s, k, j):
                if isinstance(s, int) and s + 3 < E:
                    e = s + 3
                    v = slice(e * H, (e + 1) * H)
                    dve.wait_ge(s_w_hi, 2 * e + 1)
                    dve.scalar_tensor_tensor(w1l[:, v], w_stage[:, 0, :], g_ws[:, e:e + 1], w1h[:, v],
                                             ALU.mult, ALU.subtract).then_inc(s_w_lo, 1)
                    dve.wait_ge(s_w_hi, 2 * e + 2)
                    dve.scalar_tensor_tensor(w2l[:, v], w_stage[:, 1, :], WS, w2h[:, v],
                                             ALU.mult, ALU.subtract).then_inc(s_w_lo, 1)
                    if e == E - 1:
                        dve.wait_ge(s_b1_mm, E)
                        dve.tensor_tensor(b1c[:, :], ps[:, 7, 0:E * HC], cols[:, 0:E * HC], ALU.add).then_inc(s_b1c, 1)
                if group(s + 1):
                    scores(s + 1, (k + 1) % 2)
                if group(s):
                    attended(s, k % 2)
                if group(s + 2):
                    first_norm(s + 2, k % 2)
                if group(s - 2):
                    logits(s - 2, k % 2, (k - 2) % 4)
                if routes(s, k):
                    c = Chain(dve, s_route, j * ROUTE, ROUTE)
                    picks(j, c)
                if group(s + 3):
                    first_stats(s + 3, (k + 3) % 2, (k + 3) % 4)
                if group(s):
                    residual(s, k % 2)
                if routes(s, k):
                    places(j, c, k, bass.ds(j * BLK, BLK))
                    c.end()
                if group(s - 5):
                    rows(s - 5, (k - 5) % 2, (k - 5) % 4)
                if group(s - 1):
                    tokens(s - 1, (k - 1) % 2, (k - 1) % 4)
            phase_a(dve, slot)

            c = Chain(dve, s_tab_chain, 0, 34)
            c(dve.tensor_copy(seen_b[:, :], seen[:, :]))
            dve.wait_ge(s_cnt_ps, 1)
            dve.memset(t0[:, 0:1], 0.0)
            dve.tensor_copy(tabs[:, 2 * NT:], ps[0:1, 7, 0:E])
            c(dve.tensor_scalar(til_i[:, :], ps[0:1, 7, 0:E], TP - 1.0, None, ALU.add))
            c(dve.tensor_scalar(til_i[:, :], til_i[:, :], TP.bit_length() - 1, None, ALU.logical_shift_right))
            c(dve.tensor_copy(til[:, :], til_i[:, :]))
            c(dve.tensor_tensor_scan(t0[:, 1:], til[:, :], zero8[:, :], 0.0, ALU.add, ALU.add))
            c(dve.tensor_scalar(jump[:, :], til[:, :], -float(TP), float(CAP), ALU.mult, ALU.add))
            c(dve.memset(ef[:, :], 0.0))
            c(dve.tensor_scalar(rf[:, :], tile_no[:, :], float(TP), None, ALU.mult))
            for e in range(1, E):
                c(dve.tensor_scalar(past[:, :], tile_no[:, :], t0[:, e:e + 1], None, ALU.is_ge))
                c(dve.tensor_tensor(ef[:, :], ef[:, :], past[:, :], ALU.add))
                c(dve.scalar_tensor_tensor(rf[:, :], past[:, :], jump[:, e - 1:e], rf[:, :], ALU.mult, ALU.add))
            c(dve.tensor_scalar(past[:, :], tile_no[:, :], t0[:, E:E + 1], None, ALU.is_lt))
            c(dve.scalar_tensor_tensor(rf[:, :], rf[:, :], -float(E * CAP), past[:, :], ALU.add, ALU.mult))
            c(dve.tensor_scalar(tabs[:, 0:NT], rf[:, :], float(E * CAP), None, ALU.add))
            c(dve.tensor_copy(tabs[:, NT:2 * NT], ef[:, :]))
            c(dve.memset(past[:, :], 0.0))
            c.end()
            dve.memset(past[:, :], 0.0).then_inc(s_tab, 1)

            def slot_b(s, k):
                t, q = s + 1, (k + 1) % 2
                if tile(t):
                    dve.wait_ge(s_gelu, t + 1)
                    if since(t, 2):
                        dve.wait_ge(s_down_ps, t - 1)
                    dve.tensor_copy(hid_h(q), hid(q)).then_inc(s_hid_hi, 1)
                    dve.wait_ge(s_hid_hi, t + 1)
                    dve.tensor_tensor(hid_l(q), hid(q), hid_h(q), ALU.subtract).then_inc(s_hid_lo, 1)
            phase_b(dve, slot_b)

            with dve.Fori(0, B // CB // 2) as i:
                for q in range(2):
                    v = bass.ds(i * 2 * CB + q * CB, CB)
                    dve.wait_ge(s_y_in[q], i * 16 + 16)
                    dve.tensor_tensor(x1[:, v, :], x1[:, v, :], y_in(q)[:, :, 0:D], ALU.add).then_inc(s_c_half, 1)
                    dve.wait_ge(s_c_half, i * 2 + (q + 1))
                    dve.tensor_tensor(x1[:, v, :], x1[:, v, :], y_in(q)[:, :, D:2 * D], ALU.add).then_inc(s_c_sum, 1)

        @block.tensor
        def _(pe):
            pe.wait_ge(s_const, 17)
            pe.wait_ge(s_w_rows, 16 * 9)
            pe.transpose(ps[:, 0, 0:50], small_rows[0:50, :], ident[0:50, 0:50]).then_inc(s_cols_T, 1)
            pe.transpose(ps[:, 1, 0:128], w_gnn[:, :], ident[:, :]).then_inc(s_wT_T, 1)
            pe.wait_ge(s_cols, 1)
            pe.wait_ge(s_wT, 1)
            pe.matmul(ps[:, 2, 0:2], w_gnnT[:, :], cols[:, 48:50], start=True, stop=True)
            pe.matmul(ps[:, 2, 2:2 + E], ones_row[:, :], br_row[:, :], start=True, stop=True).then_inc(s_wa_mm, 1)
            pe.wait_ge(s_reps, 1)

            def transposes(dst, src, q):
                for b in range(GB):
                    last = pe.transpose(dst[:, b, :], src[:, q, b, :], ident[:, :])
                return last

            def slot(s, k, j):
                if isinstance(s, int) and s + 3 < E:
                    e = s + 3
                    pe.wait_ge(s_w_staged, 16 * (2 * e + 1))
                    for c in range(HC):
                        last = pe.matmul(ps[:, 7, e * HC + c:e * HC + c + 1], w_stage[:, 0, c * 128:(c + 1) * 128],
                                         cols[:, 40 + e:41 + e], start=True, stop=True)
                    last.then_inc(s_b1_mm, 1)
                g, q = s + 2, k % 2
                if group(g):
                    pe.wait_ge(s_h, g + 1)
                    if since(g, 1):
                        pe.wait_ge(s_hT, g)
                    transposes(ps_hT, h, q).then_inc(s_hT_ps, 1)
                g, q = s + 1, (k + 1) % 2
                if group(g):
                    pe.wait_ge(s_p, g + 1)
                    if since(g, 1):
                        pe.wait_ge(s_pT, g)
                    transposes(ps_pT, p, q).then_inc(s_pT_ps, 1)
                g, q = s + 2, k % 2
                if group(g):
                    pe.wait_ge(s_hT, g + 1)
                    if since(g, 1):
                        pe.wait_ge(s_wh, g)
                    for b in range(GB):
                        last = pe.matmul(ps_wh[:, b, :], hT[:, q, b, :], w_gnn[:, :], start=True, stop=True)
                    last.then_inc(s_wh_ps, 1)
                    if since(g, 1):
                        pe.wait_ge(s_e, g)
                    for b in range(GB):
                        pe.matmul(ps_s[:, b, :], wa2_rep[:, :], hT[:, q, b, :], start=True, stop=False)
                        last = pe.matmul(ps_s[:, b, :], hT[:, q, b, :], wa1_rep[:, :], start=False, stop=True)
                    last.then_inc(s_s_ps, 1)
                g, q = s + 1, (k + 1) % 2
                if group(g):
                    pe.wait_ge(s_pT, g + 1)
                    pe.wait_ge(s_wh, g + 1)
                    if since(g, 1):
                        pe.wait_ge(s_hp, g)
                    for b in range(GB):
                        last = pe.matmul(ps_att[:, b, :], pT[:, q, b, :], wh[:, q, b, :], start=True, stop=True)
                    last.then_inc(s_att_ps, 1)
                if routes(s, k):
                    pe.wait_ge(s_seen, j + 1)
                    pe.wait_ge(s_both, j + 1)
                    pe.wait_ge(s_b1c, 1)
                    if not (isinstance(j, int) and j == 0):
                        if since(j, 1):
                            pe.wait_ge(s_route, j * ROUTE)
                    pe.matmul(ps_r, ones_b[:, :], seen_b[:, :].unsqueeze(1).to_broadcast([128, BLK, E]),
                              start=True, stop=False)
                    for b in range(BLK - 1):
                        pe.matmul(ps_r[:, b + 1:BLK, :], ones_b[:, :],
                                  both[:, b:b + 1, :].to_broadcast([128, BLK - 1 - b, E]),
                                  start=False, stop=False)
                    last = pe.matmul(ps_r, tri_b[:, :], both[:, :, :], start=False, stop=True)
                    last.then_inc(s_rank_ps, 1)
                g, q = s - 1, (k - 1) % 2
                if group(g):
                    pe.wait_ge(s_xn, g + 1)
                    if since(g, 1):
                        pe.wait_ge(s_xT, g)
                    transposes(ps_xT, xn, q).then_inc(s_xT_ps, 1)
                    pe.wait_ge(s_xT, g + 1)
                    if since(g, 1):
                        pe.wait_ge(s_l, g)
                    for b in range(GB):
                        last = pe.matmul(ps_l[:, b, :], xnT[:, q, b, :], wr[:, :], start=True, stop=True)
                    last.then_inc(s_l_ps, 1)
            phase_a(pe, slot)
            pe.wait_ge(s_tab_chain, 1)
            pe.matmul(ps[:, 7, 0:E], ones_b[:, :], seen_b[:, :], start=True, stop=True).then_inc(s_cnt_ps, 1)
            pe.wait_ge(s_b2_moved, 32)
            pe.wait_ge(s_tab, 1)

            def slot_b(s, k):
                t, q, kr = s + 2, k % 2, (k + 2) % RB
                if tile(t):
                    pe.wait_ge(s_rows_in[kr], (t - kr) * (16 // RB) + 16)
                    if since(t, 2):
                        pe.wait_ge(s_rT, t - 1)
                    for part in range(2):
                        for c in range(2):
                            n = part * 2 + c
                            last = pe.transpose(ps_rT(q)[:, n * 128:(n + 1) * 128],
                                                row_in[:, kr, c, part * (D // 2):(part + 1) * (D // 2)].bitcast(F16), ident16[:, :])
                    last.then_inc(s_rT_ps, 1)
                t, q = s + 1, (k + 1) % 2
                if tile(t):
                    e = pe.value_load(tabs[0:1, bass.ds(t + NT, 1)], min_val=0, max_val=E - 1)
                    pe.wait_ge(s_rT, t + 1)
                    if since(t, 2):
                        pe.wait_ge(s_gelu, t - 1)
                    for c in range(HC):
                        v = bass.ds(e * H + c * 128, 128)
                        pe.matmul(ps_up(q)[:, c, :], w1h[:, v], rT[:, q, 0:TP], start=True, stop=False)
                        pe.matmul(ps_up(q)[:, c, :], w1h[:, v], rT[:, q, TP:], start=False, stop=False)
                        last = pe.matmul(ps_up(q)[:, c, :], w1l[:, v], rT[:, q, 0:TP], start=False, stop=True)
                    last.then_inc(s_up_ps, 1)
                t, q = s, k % 2
                if tile(t):
                    e = pe.value_load(tabs[0:1, bass.ds(t + NT, 1)], min_val=0, max_val=E - 1)
                    pe.wait_ge(s_hid_lo, t + 1)
                    if since(t, 2):
                        pe.wait_ge(s_yw, t - 1)
                    pe.matmul(ps_y(q), ones2[:, :], b2_hl[:, bass.ds(e * D, D)].unsqueeze(1).to_broadcast([2, 2, D]),
                              start=True, stop=False)
                    for c in range(HC):
                        v = bass.ds(e * H + c * D, D)
                        for part, w in ((hid_h, w2h), (hid_l, w2h), (hid_h, w2l)):
                            for half in range(2):
                                last = pe.matmul(ps_y(q)[:, half, :], part(q)[:, c, half * 128:(half + 1) * 128], w[:, v],
                                                 start=False, stop=c == HC - 1 and w is w2l and half == 1)
                    last.then_inc(s_down_ps, 1)
            phase_b(pe, slot_b)


_INS = ['x', 'adj', 'L0_gnn_W', 'L0_gnn_a', 'L0_ffn_Wr', 'L0_ffn_br', 'L0_ffn_ln_g', 'L0_ffn_ln_b', 'L0_ffn_W1',
        'L0_ffn_b1', 'L0_ffn_W2', 'L0_ffn_b2']
_OUTS = [((B, N, D), 'float32')]


def kernel(**inputs):
    import numpy as _np
    import concourse.bacc as _bacc
    from concourse import mybir as _mybir
    from concourse.bass_utils import run_bass_kernel_spmd as _run

    nc = _bacc.Bacc("TRN2", target_bir_lowering=False, num_devices=1)
    arrays, args = {}, []
    for name in _INS:
        v = _np.ascontiguousarray(inputs[name])
        arrays[f"in_{name}_dram"] = v
        args.append(nc.dram_tensor(f"in_{name}_dram", v.shape, _mybir.dt.from_np(v.dtype), kind="ExternalInput").ap())
    for i, (shape, dtype) in enumerate(_OUTS):
        dt = _mybir.dt.from_np(_np.dtype(dtype))
        args.append(nc.dram_tensor(f"out_{i}_dram", shape, dt, kind="ExternalOutput").ap())
    program(nc, *args)
    r = _run(nc, [arrays], core_ids=[0])
    got = tuple(r.results[0][f"out_{i}_dram"] for i in range(len(_OUTS)))
    return got[0]
```

```python
import concourse.bass as bass
from concourse import mybir
from contextlib import ExitStack

F32 = mybir.dt.float32
F16 = mybir.dt.float16
BF16 = mybir.dt.bfloat16
I32 = mybir.dt.int32
ALU = mybir.AluOpType
ACT = mybir.ActivationFunctionType
AXX = mybir.AxisListType.X

B, N, D = 128, 128, 128
E, H = 8, 512
HC = H // 128
GB = 4
NG = B // GB
CB = 8
BLK = 4 * GB
PAIRS = 2 * B * N
TP = 512
TC = TP // 128
NT = PAIRS // TP + E
RB, YB = 4, 2
CAP = B * N + TP
META = 4
ROW = D + META
EPS = 1e-5
ROUTE = 20
SLOPE = 0.2
NEG = -1e30
WS = 64.0


def program(nc, x, adj, W, a, Wr, br, ln_g, ln_b, W1, b1, W2, b2, out):
    ctx = ExitStack()
    with ctx:
        def sb(name, shape, dt=F32):
            return ctx.enter_context(nc.sbuf_tensor(name, shape, dt))

        def sem(name):
            return ctx.enter_context(nc.semaphore(name))

        rows_d = nc.dram_tensor("rows_d", [E * CAP + TP, ROW], I32).ap()
        y_d = nc.dram_tensor("y_d", [PAIRS, D], F32).ap()

        ps = ctx.enter_context(nc.psum_tensor("ps", [128, 8, 512], F32))

        def bank(n):
            return ps[:, n, :].rearrange("p (b d) -> p b d", b=GB)
        ps_hT, ps_wh, ps_s, ps_pT, ps_att, ps_xT = (bank(n) for n in range(6))
        ps_l = ps[:, 6, 0:GB * E].rearrange("p (b e) -> p b e", e=E)
        ps_r = ps[:, 7, 0:BLK * E].rearrange("p (b e) -> p b e", e=E)

        ident = sb("ident", [128, 128])
        ident16 = sb("ident16", [128, 128], F16)
        ones_b = sb("ones_b", [128, 128], BF16)
        tri_b = sb("tri_b", [128, 128], BF16)
        ones2 = sb("ones2", [2, 128], F16)
        rev = sb("rev", [128, E])
        ecap = sb("ecap", [128, E])
        ids = sb("ids", [128, B], I32)
        pad = sb("pad", [128, ROW], I32)
        tile_no = sb("tile_no", [128, NT])
        iota_i = sb("iota_i", [128, 2 * E + NT], I32)
        zero8 = sb("zero8", [128, E])
        adj_i = sb("adj_i", [128, 128], I32)
        mask_bias = sb("mask_bias", [128, 128])
        mask_b = sb("mask_b", [128, 128], BF16)
        ident_b = sb("ident_b", [128, 128], BF16)
        w_gnn = sb("w_gnn", [128, 128])
        w_gnnT = sb("w_gnnT", [128, 128])
        small_rows = sb("small_rows", [64, 128])
        cols = sb("cols", [128, 64])
        wa = sb("wa", [128, 2])
        wa1_rep = sb("wa1_rep", [128, 128])
        wa2_rep = sb("wa2_rep", [128, 128])
        wr = sb("wr", [128, E])
        br_row = sb("br_row", [1, E])
        br_rep = sb("br_rep", [128, E])
        ones_row = sb("ones_row", [1, 128])
        g_ws = sb("g_ws", [128, E])
        w_stage = sb("w_stage", [128, 2, H])
        w1h = sb("w1h", [128, E * H], F16)
        w1l = sb("w1l", [128, E * H], F16)
        w2h = sb("w2h", [128, E * H], F16)
        w2l = sb("w2l", [128, E * H], F16)
        b1c = sb("b1c", [128, E * HC])
        b2_f = sb("b2_f", [1, E * D])
        b2_h = sb("b2_h", [1, E * D], F16)
        b2_l = sb("b2_l", [1, E * D], F16)
        b2_hl = sb("b2_hl", [2, E * D], F16)
        arena = sb("arena", [128, 10 * 2 * GB * 128])
        h, hT, wh, e_sc, p, pT, hp, ex, xn, xnT = (
            arena[:, n * 2 * GB * 128:(n + 1) * 2 * GB * 128].rearrange("p (a b d) -> p a b d", a=2, b=GB)
            for n in range(10))
        x1 = sb("x1", [128, B, D])
        xhl = sb("xhl", [128, 4, GB, 2 * D], F16)
        st1 = sb("st1", [128, 2, GB, 6])
        mv1 = sb("mv1", [128, 2, GB, 2])
        nbias1 = sb("nbias1", [128, 2, GB])
        nmx = sb("nmx", [128, 2, GB])
        sm = sb("sm", [128, 2, GB])
        rsm = sb("rsm", [128, 2, GB])
        st2 = sb("st2", [128, 2, GB, 6])
        mv2 = sb("mv2", [128, 2, GB, 2])
        veps = sb("veps", [128, 2, 3 * GB])
        ln_v = sb("ln_v", [128, 3 * GB])
        rinv0 = sb("rinv0", [128, 3 * GB])
        newton = sb("newton", [128, 3 * GB])
        rinv = sb("rinv", [128, 2, 3 * GB])
        rec2 = sb("rec2", [128, 2, GB])
        rtot = sb("rtot", [128, 2, GB])
        nbias2 = sb("nbias2", [128, 2, GB])
        unsc = sb("unsc", [128, 2, GB])
        lg = sb("lg", [128, BLK, E])
        lg2 = sb("lg2", [128, BLK, E])
        eq = sb("eq", [128, BLK, E])
        top1 = sb("top1", [128, BLK])
        top2 = sb("top2", [128, BLK])
        pick = sb("pick", [128, 2, BLK])
        oh1 = sb("oh1", [128, BLK, E])
        oh2 = sb("oh2", [128, BLK, E])
        both = sb("both", [128, BLK, E], BF16)
        blk_sum = sb("blk_sum", [128, E])
        seen = sb("seen", [128, E])
        seen_b = sb("seen_b", [128, E], BF16)
        gap = sb("gap", [128, BLK])
        egap = sb("egap", [128, BLK])
        den = sb("den", [128, BLK])
        rk = sb("rk", [128, BLK, E])
        pos = sb("pos", [128, 2, BLK])
        meta = sb("meta", [128, BLK, META])
        row_out = sb("row_out", [128, 2, GB, ROW], I32)
        idx = sb("idx", [128, 2, 2 * GB], I32)
        til_i = sb("til_i", [128, E], I32)
        til = sb("til", [128, E])
        t0 = sb("t0", [128, E + 1])
        jump = sb("jump", [128, E])
        past = sb("past", [128, NT])
        rf = sb("rf", [128, NT])
        ef = sb("ef", [128, NT])
        code = sb("code", [128, NT])
        tabs = sb("tabs", [1, 2 * NT + E], I32)
        row_in = sb("row_in", [128, RB, TC, ROW], I32)
        rT = sb("rT", [128, 2, 2 * TP], F16)
        yw = sb("yw", [128, YB, TC, D])
        is_first = sb("is_first", [128, TC])
        w_sel = sb("w_sel", [128, RB, TC])
        y_idx = sb("y_idx", [128, RB, TC], I32)

        s_const = sem("s_const")
        s_w_rows = sem("s_w_rows")
        s_cols_T = sem("s_cols_T")
        s_cols = sem("s_cols")
        s_wT_T = sem("s_wT_T")
        s_wT = sem("s_wT")
        s_wa_mm = sem("s_wa_mm")
        s_wa = sem("s_wa")
        s_reps = sem("s_reps")
        s_prep = sem("s_prep")
        s_w_staged = sem("s_w_staged")
        s_w_hi = sem("s_w_hi")
        s_w_lo = sem("s_w_lo")
        s_b1_mm = sem("s_b1_mm")
        s_b1c = sem("s_b1c")
        s_b2_parts = sem("s_b2_parts")
        s_b2_moved = sem("s_b2_moved")
        s_x_in = sem("s_x_in")
        s_veps_set = sem("s_veps_set")
        s_stats1 = sem("s_stats1")
        s_aggr1 = sem("s_aggr1")
        s_veps1 = sem("s_veps1")
        s_ln = sem("s_ln")
        s_rinv0 = sem("s_rinv0")
        s_newton = sem("s_newton")
        s_rinv = sem("s_rinv")
        s_sel = sem("s_sel")
        s_nbias1 = sem("s_nbias1")
        s_h = sem("s_h")
        s_hT_ps = sem("s_hT_ps")
        s_hT = sem("s_hT")
        s_wh_ps = sem("s_wh_ps")
        s_wh = sem("s_wh")
        s_s_ps = sem("s_s_ps")
        s_relu = sem("s_relu")
        s_leaky = sem("s_leaky")
        s_nmx = sem("s_nmx")
        s_p = sem("s_p")
        s_pT_ps = sem("s_pT_ps")
        s_pT = sem("s_pT")
        s_att_ps = sem("s_att_ps")
        s_rsm = sem("s_rsm")
        s_rtot = sem("s_rtot")
        s_hp = sem("s_hp")
        s_ex = sem("s_ex")
        s_elu = sem("s_elu")
        s_x1 = sem("s_x1")
        s_stats2 = sem("s_stats2")
        s_aggr2 = sem("s_aggr2")
        s_vq_chain = sem("s_vq_chain")
        s_vq = sem("s_vq")
        s_scales = sem("s_scales")
        s_xn = sem("s_xn")
        s_xn_hi = sem("s_xn_hi")
        s_xn_lo = sem("s_xn_lo")
        s_xT_ps = sem("s_xT_ps")
        s_xT = sem("s_xT")
        s_l_ps = sem("s_l_ps")
        s_l = sem("s_l")
        s_route = sem("s_route")
        s_gap = sem("s_gap")
        s_egap = sem("s_egap")
        s_both = sem("s_both")
        s_seen = sem("s_seen")
        s_rank_ps = sem("s_rank_ps")
        s_rows = sem("s_rows")
        s_cnt_ps = sem("s_cnt_ps")
        s_tab_chain = sem("s_tab_chain")
        s_tab = sem("s_tab")
        s_pads = sem("s_pads")
        s_rT_ps = sem("s_rT_ps")
        s_rT = sem("s_rT")
        s_up_ps = sem("s_up_ps")
        s_gelu = sem("s_gelu")
        s_hid_hi = sem("s_hid_hi")
        s_hid_lo = sem("s_hid_lo")
        s_down_ps = sem("s_down_ps")
        s_yw = sem("s_yw")
        s_c_half = sem("s_c_half")
        s_c_sum = sem("s_c_sum")
        s_stored = sem("s_stored")
        s_scat = [sem(f"s_scat{n}") for n in range(2)]
        s_rows_in = [sem(f"s_rows_in{n}") for n in range(RB)]
        s_y_out = [sem(f"s_y_out{n}") for n in range(YB)]
        s_y_in = [sem(f"s_y_in{n}") for n in range(2)]

        def since(n, first):
            return not isinstance(n, int) or n >= first

        class Chain:
            def __init__(self, eng, sem, base, steps):
                self.eng, self.sem, self.base, self.steps, self.n = eng, sem, base, steps, 0

            def __call__(self, ins):
                self.n += 1
                ins.then_inc(self.sem, 1)
                self.eng.wait_ge(self.sem, self.base + self.n)

            def end(self):
                assert self.n == self.steps, self.n

        def group(g):
            return not isinstance(g, int) or 0 <= g < NG

        def of(g, b=None):
            return bass.ds(g * GB, GB) if b is None else bass.ds(g * GB + b, 1)

        def x1_of(g, b):
            return x1[:, of(g, b), :].rearrange("p a d -> p (a d)")

        LOOP_A = 8
        TURNS_A = (NG - 4 - LOOP_A) // 4

        def phase_a(eng, slot):
            for s in range(-4, LOOP_A):
                slot(s, s % 4, (s - 5) // 4)
            with eng.Fori(0, TURNS_A) as i:
                for k in range(4):
                    slot(i * 4 + (LOOP_A + k), (LOOP_A + k) % 4, i + (LOOP_A - 4) // 4)
            for s in range(LOOP_A + 4 * TURNS_A, NG + 5):
                slot(s, s % 4, (s - 5) // 4)

        def routes(s, k):
            return k == 1 and not (isinstance(s, int) and s < 5)

        FIRST_B = RB
        TURNS_B = (NT - FIRST_B - 2) // RB

        def phase_b(eng, slot):
            for s in range(-2, FIRST_B):
                slot(s, s % RB)
            with eng.Fori(0, TURNS_B) as i:
                for k in range(RB):
                    slot(i * RB + (FIRST_B + k), k)
            for s in range(FIRST_B + RB * TURNS_B, NT):
                slot(s, s % RB)

        def tile(t):
            return not isinstance(t, int) or 0 <= t < NT

        def ps_rT(q):
            return ps[:, q, :].bitcast(F16)

        ps_up = ps[:, 2:6, :]

        def ps_y(q):
            return ps[:, 6 + q, :].rearrange("p (s d) -> p s d", s=TC)

        def hid(q):
            return arena[:, q * HC * TP:(q + 1) * HC * TP].rearrange("p (c t) -> p c t", c=HC)

        def part_of(n):
            first = 2 * HC * TP + n * HC * TP // 2
            return arena[:, first:first + HC * TP // 2].bitcast(F16).rearrange("p (c t) -> p c t", c=HC)

        def hid_h(q):
            return part_of(2 * q)

        def hid_l(q):
            return part_of(2 * q + 1)


        def y_in(q):
            return (w1h, w1l)[q][:, :].bitcast(F32).rearrange("p (b d) -> p b d", b=CB)

        block = ctx.enter_context(nc.Block())

        @block.sync
        def _(sp):
            xv = x.rearrange("b n d -> n b d")

            def load_x(i):
                if since(i, 1):
                    sp.wait_ge(s_x_in, i * 16)
                v = bass.ds(i * CB, CB)
                sp.dma_start(x1[:, v, :], xv[:, v, :]).then_inc(s_x_in, 16)

            load_x(0)
            load_x(1)
            for dst, src in [(adj_i[:, :], adj), (w_gnn[:, :], W), (wr[:, :], Wr),
                             (br_row[:, :], br.rearrange("(o e) -> o e", o=1)),
                             (small_rows[0:32, :], b1.rearrange("e (c p) -> (e c) p", p=128)),
                             (small_rows[32:40, :], ln_g), (small_rows[40:48, :], ln_b),
                             (small_rows[48:50, :], a.rearrange("(r p) o -> r (p o)", r=2)),
                             (b2_f[:, :], b2.rearrange("(o e) d -> o (e d)", o=1))]:
                sp.dma_start(dst, src).then_inc(s_w_rows, 16)
            for n in range(2 * E):
                if n >= 1:
                    sp.wait_ge(s_w_staged, 16 * n)
                if n >= 2:
                    sp.wait_ge(s_w_lo, n - 1)
                if n >= 2 and n % 2 == 0:
                    sp.wait_ge(s_b1_mm, n // 2)
                if n % 2 == 0:
                    src, dst = W1[n // 2], w_stage[:, 0, :]
                else:
                    src = W2[n // 2].rearrange("(c p) d -> p c d", p=128)
                    dst = w_stage[:, 1, :].rearrange("p (c d) -> p c d", c=HC)
                sp.dma_start(dst, src).then_inc(s_w_staged, 16)
                if n in (5, 9):
                    load_x(2 if n == 5 else 3)
            sp.wait_ge(s_b2_parts, 2)
            sp.dma_start(b2_hl[0:1, :], b2_h[:, :]).then_inc(s_b2_moved, 16)
            sp.dma_start(b2_hl[1:2, :], b2_l[:, :]).then_inc(s_b2_moved, 16)
            with sp.Fori(4, B // CB) as i:
                load_x(i)

            sp.wait_ge(s_tab, 1)
            for q in range(2):
                sp.wait_ge(s_scat[q], 128 * (NG // 2))
            no_pair = pad[:, :].rearrange("p (c r) -> p c r", c=1).to_broadcast([128, TP // 128, ROW])
            for e in range(E):
                n_e = sp.value_load(tabs[0:1, 2 * NT + e:2 * NT + e + 1], min_val=0, max_val=B * N)
                sp.dma_start(rows_d[bass.ds(n_e + e * CAP, TP), :].rearrange("(c p) r -> p c r", p=128),
                             no_pair).then_inc(s_pads, 16)
            sp.dma_start(rows_d[E * CAP:E * CAP + TP, :].rearrange("(c p) r -> p c r", p=128),
                         no_pair).then_inc(s_pads, 16)
            sp.wait_ge(s_pads, 16 * (E + 1))

            def load_rows(t, k):
                r = sp.value_load(tabs[0:1, bass.ds(t, 1)], min_val=0, max_val=E * CAP)
                sp.dma_start(row_in[:, k, :, :], rows_d[bass.ds(r, TP), :].rearrange("(c p) r -> p c r", p=128))\
                    .then_inc(s_rows_in[k], 16)

            for k in range(RB):
                load_rows(k, k)
            with sp.Fori(1, NT // RB) as i:
                for k in range(RB):
                    sp.wait_ge(s_sel, i * (3 * RB) + 3 * (k - RB + 1))
                    load_rows(i * RB + k, k)

            for q in range(YB):
                sp.wait_ge(s_y_out[q], 16 * TC * NT // YB)
            yv = y_d.rearrange("(b n k) d -> n b (k d)", n=N, k=2)
            ov = out.rearrange("b n d -> n b d")

            def load_y(c, q):
                sp.dma_start(y_in(q), yv[:, bass.ds(c * CB, CB), :]).then_inc(s_y_in[q], 16)

            def store(c):
                sp.wait_ge(s_c_sum, c + 1)
                v = bass.ds(c * CB, CB)
                sp.dma_start(ov[:, v, :], x1[:, v, :]).then_inc(s_stored, 16)

            for q in range(2):
                load_y(q, q)
            with sp.Fori(0, B // CB // 2 - 1) as i:
                for q in range(2):
                    store(i * 2 + q)
                    load_y(i * 2 + (2 + q), q)
            for q in range(2):
                store(B // CB - 2 + q)
            sp.wait_ge(s_stored, 16 * (B // CB))

        @block.gpsimd
        def _(pool):
            for t, v in ((ident, 0.0), (tri_b, 1.0), (ones_b, 1.0), (ones2, 1.0), (ones_row, 1.0),
                         (seen, 0.0), (zero8, 0.0)):
                pool.memset(t[:, :], v).then_inc(s_const, 1)
            pool.memset(pad[:, 0:D], 0).then_inc(s_const, 1)
            pool.memset(pad[:, D:D + 1].bitcast(F32), PAIRS + 1.0).then_inc(s_const, 1)
            pool.memset(pad[:, D + 1:ROW], 0).then_inc(s_const, 1)
            pool.iota(ids[:, :], pattern=[[2 * N, B]], base=1, channel_multiplier=2).then_inc(s_const, 1)
            pool.iota(iota_i[:, 0:E], pattern=[[-1, E]], base=E, channel_multiplier=0).then_inc(s_const, 1)
            pool.iota(iota_i[:, E:2 * E], pattern=[[CAP, E]], base=0, channel_multiplier=0).then_inc(s_const, 1)
            pool.iota(iota_i[:, 2 * E:], pattern=[[1, NT]], base=0, channel_multiplier=0).then_inc(s_const, 1)
            pool.wait_ge(s_const, 14)
            pool.affine_select(out=ident[:, :], in_=ident[:, :], compare_op=ALU.not_equal, fill=1.0, base=0,
                               pattern=[[-1, 128]], channel_multiplier=1).then_inc(s_const, 1)
            pool.affine_select(out=tri_b[:, :], in_=tri_b[:, :], compare_op=ALU.is_gt, fill=0.0, base=0,
                               pattern=[[1, 128]], channel_multiplier=-1).then_inc(s_const, 1)

            def slot(s, k, j):
                g, q = s - 5, (k - 5) % 2
                if group(g):
                    pool.wait_ge(s_rows, g + 1)
                    pool.nop(nofuse=True)
                    for n in range(2 * GB):
                        pool.indirect_dma_start(
                            rows_d[:, :], bass.IndirectOffsetOnAxis(ap=idx[:, q, n:n + 1], axis=0),
                            row_out[:, q, n % GB, :], None).then_inc(s_scat[q], 16)
            phase_a(pool, slot)

            def slot_b(s, k):
                if tile(s) and not (isinstance(s, int) and s < 0):
                    pool.wait_ge(s_yw, s + 1)
                    pool.nop(nofuse=True)
                    for c in range(TC):
                        pool.indirect_dma_start(
                            y_d[:, :],
                            bass.IndirectOffsetOnAxis(ap=y_idx[:, k, c:c + 1], axis=0),
                            yw[:, k % YB, c, :], None, bounds_check=PAIRS - 1,
                            oob_is_err=False).then_inc(s_y_out[k % YB], 16)
            phase_b(pool, slot_b)

        @block.scalar
        def _(act):
            def slot(s, k, j):
                if isinstance(s, int) and 0 <= s + 3 < E:
                    e = s + 3
                    act.wait_ge(s_cols, 2)
                    act.wait_ge(s_w_staged, 16 * (2 * e + 1))
                    act.activation(w1h[:, e * H:(e + 1) * H], w_stage[:, 0, :], ACT.Copy,
                                   scale=g_ws[:, e:e + 1]).then_inc(s_w_hi, 1)
                    act.wait_ge(s_w_staged, 16 * (2 * e + 2))
                    act.activation(w2h[:, e * H:(e + 1) * H], w_stage[:, 1, :], ACT.Copy, scale=WS).then_inc(s_w_hi, 1)
                if group(s + 3) or group(s - 1):
                    if group(s + 3):
                        act.wait_ge(s_veps1, s + 4)
                    if group(s - 1):
                        act.wait_ge(s_vq, s)
                    act.activation(ln_v[:, :], veps[:, (k + 1) % 2, :], ACT.Ln).then_inc(s_ln, 1)
                    act.wait_ge(s_ln, s + 4)
                    act.activation(rinv0[:, :], ln_v[:, :], ACT.Exp, scale=-0.5).then_inc(s_rinv0, 1)
                g, q = s + 2, k % 2
                if group(g):
                    act.wait_ge(s_wh_ps, g + 1)
                    if since(g, 2):
                        act.wait_ge(s_att_ps, g - 1)
                    act.copy(wh[:, q, :, :], ps_wh).then_inc(s_wh, 1)
                g, q = s, k % 2
                if group(g):
                    act.wait_ge(s_hp, g + 1)
                    act.activation(ex[:, q, :, :], hp[:, q, :, :], ACT.Exp).then_inc(s_ex, 1)
                g, q = s + 2, k % 2
                if group(g):
                    act.wait_ge(s_s_ps, g + 1)
                    if since(g, 2):
                        act.wait_ge(s_leaky, g - 1)
                    act.activation(e_sc[:, q, :, :], ps_s, ACT.Relu, scale=SLOPE - 1.0).then_inc(s_relu, 1)
                g, q = s + 1, (k + 1) % 2
                if group(g):
                    act.wait_ge(s_nmx, g + 1)
                    for b in range(GB):
                        last = act.activation(p[:, q, b, :], p[:, q, b, :], ACT.Exp, bias=nmx[:, q, b:b + 1],
                                              accum_out=sm[:, q, b:b + 1])
                    last.then_inc(s_p, 1)
                g, q = s + 3, (k + 3) % 2
                if group(g):
                    act.wait_ge(s_nbias1, g + 1)
                    if since(g, 2):
                        act.wait_ge(s_hT_ps, g - 1)
                    act.nop(nofuse=True)
                    for b in range(GB):
                        last = act.activation(h[:, q, b, :], x1_of(g, b), ACT.Identity, bias=nbias1[:, q, b:b + 1],
                                              scale=rinv[:, q, b:b + 1])
                    last.then_inc(s_h, 1)
                if routes(s, k):
                    act.wait_ge(s_gap, j + 1)
                    act.activation(egap[:, :], gap[:, :], ACT.Exp).then_inc(s_egap, 1)
                g, q = s + 1, (k + 1) % 2
                if group(g):
                    act.wait_ge(s_pT_ps, g + 1)
                    if since(g, 2):
                        act.wait_ge(s_att_ps, g - 1)
                    act.copy(pT[:, q, :, :], ps_pT).then_inc(s_pT, 1)
                g, q = s - 1, (k - 1) % 2
                if group(g):
                    act.wait_ge(s_scales, g + 1)
                    if since(g, 2):
                        act.wait_ge(s_xT_ps, g - 1)
                        act.wait_ge(s_xn_lo, g - 1)
                    act.nop(nofuse=True)
                    for b in range(GB):
                        last = act.activation(xn[:, q, b, :], x1_of(g, b), ACT.Identity, bias=nbias2[:, q, b:b + 1],
                                              scale=rtot[:, q, b:b + 1])
                    last.then_inc(s_xn, 1)
                g, q = s + 3, (k + 3) % 2
                if group(g):
                    act.wait_ge(s_hT_ps, g + 1)
                    if since(g, 2):
                        act.wait_ge(s_s_ps, g - 1)
                    act.copy(hT[:, q, :, :], ps_hT).then_inc(s_hT, 1)
                g, q = s - 1, (k - 1) % 2
                if group(g):
                    act.wait_ge(s_xT_ps, g + 1)
                    if since(g, 2):
                        act.wait_ge(s_l_ps, g - 1)
                    act.copy(xnT[:, q, :, :], ps_xT).then_inc(s_xT, 1)
            phase_a(act, slot)
            act.wait_ge(s_tab, 1)

            def slot_b(s, k):
                t, q = s + 2, k % 2
                if tile(t):
                    act.wait_ge(s_rT_ps, t + 1)
                    if since(t, 2):
                        act.wait_ge(s_up_ps, 2 * t - 2)
                    act.copy(rT[:, q, :], ps_rT(q)).then_inc(s_rT, 1)
                t, q = s + 1, (k + 1) % 2
                if tile(t):
                    e = act.value_load(tabs[0:1, bass.ds(t + NT, 1)], min_val=0, max_val=E - 1)
                    if since(t, 2):
                        act.wait_ge(s_hid_lo, 2 * t - 2)
                    for half in range(2):
                        act.wait_ge(s_up_ps, 2 * t + (half + 1))
                        act.nop(nofuse=True)
                        for c in range(half * HC // 2, (half + 1) * HC // 2):
                            last = act.activation(hid(q)[:, c, :], ps_up[:, c, :], ACT.Gelu,
                                                  bias=b1c[:, bass.ds(e * HC + c, 1)], scale=1.0 / WS)
                        last.then_inc(s_gelu, 1)
                t, q = s, k % 2
                if tile(t):
                    act.wait_ge(s_down_ps, t + 1)
                    act.wait_ge(s_sel, 3 * t + 3)
                    r = k % YB
                    if since(t, YB):
                        act.wait_ge(s_y_out[r], (t - r) * (16 * TC // YB))
                    for c in range(TC):
                        last = act.activation(yw[:, r, c, :], ps_y(q)[:, c, :], ACT.Copy,
                                              scale=w_sel[:, k, c:c + 1])
                    last.then_inc(s_yw, 1)
            phase_b(act, slot_b)

        @block.vector
        def _(dve):
            def spread(ap, shape, dim):
                return ap.unsqueeze(dim).to_broadcast(shape)

            dve.wait_ge(s_const, 16)
            dve.tensor_copy(ident16[:, :], ident[:, :])
            dve.tensor_copy(rev[:, :], iota_i[:, 0:E])
            dve.tensor_copy(ecap[:, :], iota_i[:, E:2 * E])
            dve.tensor_copy(tile_no[:, :], iota_i[:, 2 * E:]).then_inc(s_prep, 1)
            dve.wait_ge(s_w_rows, 16 * 9)
            prep = Chain(dve, s_prep, 1, 4)
            prep(dve.tensor_scalar(mask_bias[:, :], adj_i[:, :], 0.0, None, ALU.is_gt))
            prep(dve.tensor_tensor(mask_bias[:, :], mask_bias[:, :], ident[:, :], ALU.max))
            prep(dve.tensor_scalar(mask_bias[:, :], mask_bias[:, :], 1.0, -NEG, ALU.subtract, ALU.mult))
            dve.tensor_copy(ident_b[:, :], ident[:, :])
            prep(dve.tensor_copy(mask_b[:, :], mask_bias[:, :]))
            prep.end()
            dve.memset(veps[:, :, :], 1.0).then_inc(s_veps_set, 1)
            dve.tensor_scalar(b2_h[:, :], b2_f[:, :], WS, None, ALU.mult).then_inc(s_b2_parts, 1)
            dve.wait_ge(s_b2_parts, 1)
            dve.scalar_tensor_tensor(b2_l[:, :], b2_f[:, :], WS, b2_h[:, :], ALU.mult, ALU.subtract).then_inc(s_b2_parts, 1)
            dve.wait_ge(s_cols_T, 1)
            dve.tensor_copy(cols[:, 0:50], ps[:, 0, 0:50]).then_inc(s_cols, 1)
            dve.wait_ge(s_cols, 1)
            dve.tensor_scalar(g_ws[:, :], cols[:, 32:40], WS, None, ALU.mult).then_inc(s_cols, 1)
            dve.wait_ge(s_wT_T, 1)
            dve.tensor_copy(w_gnnT[:, :], ps[:, 1, 0:128]).then_inc(s_wT, 1)
            dve.wait_ge(s_wa_mm, 1)
            dve.tensor_copy(br_rep[:, :], ps[:, 2, 2:2 + E])
            dve.tensor_copy(wa[:, :], ps[:, 2, 0:2]).then_inc(s_wa, 1)
            dve.wait_ge(s_wa, 1)
            dve.tensor_copy(wa1_rep[:, :], wa[:, 0:1].to_broadcast([128, 128]))
            dve.tensor_copy(wa2_rep[:, :], wa[:, 1:2].to_broadcast([128, 128])).then_inc(s_reps, 1)

            def stats(g, q, st, s_stats):
                dve.nop(nofuse=True)
                for b in range(GB):
                    last = dve.bn_stats(st[:, q, b, :], x1_of(g, b))
                last.then_inc(s_stats, 1)

            def mean_variance(g, q, st, mv, s_stats, s_aggr):
                dve.wait_ge(s_stats, g + 1)
                dve.nop(nofuse=True)
                for b in range(GB):
                    last = dve.bn_aggr(mv[:, q, b, :], st[:, q, b, :])
                last.then_inc(s_aggr, 1)

            ALLE = [128, BLK, E]

            def picks(j, c):
                dve.wait_ge(s_l, j * 4 + 4)
                c(dve.tensor_tensor(lg[:, :, :], lg[:, :, :], spread(br_rep[:, :], ALLE, 1), ALU.add))
                for src, top, oh, n in ((lg, top1, oh1, 0), (lg2, top2, oh2, 1)):
                    c(dve.tensor_reduce(top[:, :], src[:, :, :], AXX, ALU.max))
                    c(dve.tensor_tensor(eq[:, :, :], src[:, :, :], spread(top[:, :], ALLE, 2), ALU.is_equal))
                    c(dve.tensor_tensor(eq[:, :, :], eq[:, :, :], spread(rev[:, :], ALLE, 1), ALU.mult))
                    c(dve.tensor_reduce(pick[:, n, :], eq[:, :, :], AXX, ALU.max))
                    c(dve.tensor_tensor(oh[:, :, :], spread(pick[:, n, :], ALLE, 2), spread(rev[:, :], ALLE, 1),
                                        ALU.is_equal))
                    if n == 0:
                        c(dve.scalar_tensor_tensor(lg2[:, :, :], oh1[:, :, :], -3e38, lg[:, :, :], ALU.mult, ALU.add))
                        dve.tensor_copy(seen_b[:, :], seen[:, :]).then_inc(s_seen, 1)
                dve.tensor_tensor(both[:, :, :], oh1[:, :, :], oh2[:, :, :], ALU.add).then_inc(s_both, 1)
                dve.tensor_tensor(gap[:, :], top2[:, :], top1[:, :], ALU.subtract).then_inc(s_gap, 1)

            def places(j, c, k, ids_of):
                dve.wait_ge(s_both, j + 1)
                c(dve.tensor_reduce(blk_sum[:, :], both[:, :, :].rearrange("p b e -> p e b"), AXX, ALU.add))
                dve.tensor_tensor(seen[:, :], seen[:, :], blk_sum[:, :], ALU.add)
                dve.wait_ge(s_egap, j + 1)
                c(dve.tensor_scalar(den[:, :], egap[:, :], 1.0, None, ALU.add))
                c(dve.reciprocal(den[:, :], den[:, :]))
                c(dve.tensor_scalar(den[:, :], den[:, :], 1.0 / WS, None, ALU.mult))
                c(dve.tensor_tensor(meta[:, :, 3], den[:, :], egap[:, :], ALU.mult))
                dve.tensor_tensor(meta[:, :, 2], den[:, :], meta[:, :, 3], ALU.subtract)
                dve.tensor_copy(meta[:, :, 1], pick[:, 0, :])
                dve.tensor_copy(meta[:, :, 0], ids[:, ids_of])
                dve.wait_ge(s_rank_ps, j + 1)
                c(dve.tensor_tensor(rk[:, :, :], ps_r, spread(ecap[:, :], ALLE, 1), ALU.add))
                dve.tensor_tensor(eq[:, :, :], rk[:, :, :], oh1[:, :, :], ALU.mult)
                c(dve.tensor_tensor(lg2[:, :, :], rk[:, :, :], oh2[:, :, :], ALU.mult))
                dve.tensor_reduce(pos[:, 0, :], eq[:, :, :], AXX, ALU.add)
                c(dve.tensor_reduce(pos[:, 1, :], lg2[:, :, :], AXX, ALU.add))

            def rows(g, q, k):
                if since(g, 2):
                    dve.wait_ge(s_scat[q], (g - q) * 64)
                dve.wait_ge(s_xn_lo, g + 1)
                dve.tensor_copy(row_out[:, q, :, 0:D].bitcast(F16), xhl[:, k, :, :])
                dve.tensor_copy(row_out[:, q, :, D:ROW].bitcast(F32), meta[:, k * GB:(k + 1) * GB, :])
                dve.tensor_copy(idx[:, q, :].rearrange("p (n b) -> p n b", n=2),
                                pos[:, :, k * GB:(k + 1) * GB]).then_inc(s_rows, 1)

            def slot(s, k, j):
                if isinstance(s, int) and 0 <= s + 3 < E:
                    e = s + 3
                    v = slice(e * H, (e + 1) * H)
                    dve.wait_ge(s_w_hi, 2 * e + 1)
                    dve.scalar_tensor_tensor(w1l[:, v], w_stage[:, 0, :], g_ws[:, e:e + 1], w1h[:, v],
                                             ALU.mult, ALU.subtract).then_inc(s_w_lo, 1)
                    dve.wait_ge(s_w_hi, 2 * e + 2)
                    dve.scalar_tensor_tensor(w2l[:, v], w_stage[:, 1, :], WS, w2h[:, v],
                                             ALU.mult, ALU.subtract).then_inc(s_w_lo, 1)
                    if e == E - 1:
                        dve.wait_ge(s_b1_mm, E)
                        dve.tensor_tensor(b1c[:, :], ps[:, 7, 0:E * HC], cols[:, 0:E * HC], ALU.add).then_inc(s_b1c, 1)
                q, q1 = k % 2, (k + 1) % 2
                if group(s):
                    dve.wait_ge(s_p, s + 1)
                    dve.reciprocal(rsm[:, q, :], sm[:, q, :]).then_inc(s_rsm, 1)
                if group(s + 1):
                    dve.wait_ge(s_relu, s + 2)
                    if since(s, 1):
                        dve.wait_ge(s_pT_ps, s)
                    dve.tensor_tensor(p[:, q1, :, :], ps_s, e_sc[:, q1, :, :], ALU.add).then_inc(s_leaky, 1)
                norms = group(s + 3) or group(s - 1)
                if norms:
                    dve.wait_ge(s_rinv0, s + 4)
                    dve.tensor_tensor(newton[:, :], rinv0[:, :], rinv0[:, :], ALU.mult).then_inc(s_newton, 1)
                if group(s):
                    dve.wait_ge(s_rsm, s + 1)
                    dve.wait_ge(s_att_ps, s + 1)
                    dve.tensor_tensor(hp[:, q, :, :], ps_att, spread(rsm[:, q, :], [128, GB, D], 2),
                                      ALU.mult).then_inc(s_hp, 1)
                if norms:
                    dve.wait_ge(s_newton, 2 * s + 7)
                    dve.scalar_tensor_tensor(newton[:, :], newton[:, :], -0.5, veps[:, q1, :],
                                             ALU.mult, ALU.mult).then_inc(s_newton, 1)
                if group(s + 1):
                    dve.wait_ge(s_leaky, s + 2)
                    dve.tensor_reduce(nmx[:, q1, :], p[:, q1, :, :], AXX, ALU.max, negate=True).then_inc(s_nmx, 1)
                if norms:
                    dve.wait_ge(s_newton, 2 * s + 8)
                    dve.scalar_tensor_tensor(rinv[:, q1, :], newton[:, :], 1.5, rinv0[:, :],
                                             ALU.add, ALU.mult).then_inc(s_rinv, 1)
                if group(s + 4):
                    dve.wait_ge(s_x_in, (s + 4 - q) * 8 + 16)
                    stats(s + 4, q, st1, s_stats1)
                if norms:
                    dve.wait_ge(s_rinv, s + 4)
                if group(s + 3):
                    dve.scalar_tensor_tensor(nbias1[:, q1, :], mv1[:, q1, :, 0], -1.0, rinv[:, q1, 0:GB],
                                             ALU.mult, ALU.mult).then_inc(s_nbias1, 1)
                if group(s - 1):
                    dve.tensor_tensor(rtot[:, q1, :], rinv[:, q1, GB:2 * GB], rinv[:, q1, 2 * GB:], ALU.mult).then_inc(s_rtot, 1)
                    dve.tensor_tensor(unsc[:, q1, :], veps[:, q1, 2 * GB:], rinv[:, q1, 2 * GB:], ALU.mult)
                if group(s - 2):
                    dve.wait_ge(s_l_ps, s - 1)
                    dve.tensor_tensor(lg[:, (k + 2) % 4 * GB:((k + 2) % 4 + 1) * GB, :], ps_l,
                                      spread(unsc[:, q, :], [128, GB, E], 2), ALU.mult).then_inc(s_l, 1)
                if group(s - 1):
                    dve.wait_ge(s_rtot, s)
                    dve.scalar_tensor_tensor(nbias2[:, q1, :], mv2[:, q1, :, 0], -1.0, rtot[:, q1, :],
                                             ALU.mult, ALU.mult).then_inc(s_scales, 1)
                if group(s + 4):
                    mean_variance(s + 4, q, st1, mv1, s_stats1, s_aggr1)
                if routes(s, k):
                    c = Chain(dve, s_route, j * ROUTE, ROUTE)
                    picks(j, c)
                if group(s):
                    dve.wait_ge(s_ex, s + 1)
                    dve.scalar_tensor_tensor(x1[:, of(s), :], ex[:, q, :, :], 1.0, x1[:, of(s), :],
                                             ALU.min, ALU.add).then_inc(s_elu, 1)
                if group(s + 4):
                    dve.wait_ge(s_aggr1, s + 5)
                    dve.tensor_scalar(veps[:, q, 0:GB], mv1[:, q, :, 1], EPS, None, ALU.add).then_inc(s_veps1, 1)
                if group(s):
                    dve.wait_ge(s_elu, s + 1)
                    dve.scalar_tensor_tensor(x1[:, of(s), :], hp[:, q, :, :], 0.0, x1[:, of(s), :],
                                             ALU.max, ALU.add).then_inc(s_x1, 1)
                    dve.wait_ge(s_x1, s + 1)
                    stats(s, q, st2, s_stats2)
                if routes(s, k):
                    places(j, c, k, bass.ds(j * BLK, BLK))
                    c.end()
                if group(s - 5):
                    rows(s - 5, q1, (k + 3) % 4)
                if group(s):
                    mean_variance(s, q, st2, mv2, s_stats2, s_aggr2)
                if group(s - 1):
                    dve.wait_ge(s_xn, s)
                    if since(s, 5):
                        dve.wait_ge(s_rows, s - 4)
                    dve.tensor_copy(xhl[:, (k + 3) % 4, :, 0:D], xn[:, q1, :, :]).then_inc(s_xn_hi, 1)
                if group(s):
                    dve.wait_ge(s_aggr2, s + 1)
                    c = Chain(dve, s_vq_chain, s * 3, 3)
                    c(dve.tensor_scalar(veps[:, q, GB:2 * GB], mv2[:, q, :, 1], EPS, None, ALU.add))
                    c(dve.reciprocal(rec2[:, q, :], veps[:, q, GB:2 * GB]))
                    c(dve.tensor_tensor(veps[:, q, 2 * GB:], rec2[:, q, :], mv2[:, q, :, 1], ALU.mult))
                    c.end()
                    dve.tensor_scalar(veps[:, q, 2 * GB:], veps[:, q, 2 * GB:], EPS, None, ALU.add).then_inc(s_vq, 1)
                if group(s - 1):
                    dve.wait_ge(s_xn_hi, s)
                    dve.tensor_tensor(xhl[:, (k + 3) % 4, :, D:2 * D], xn[:, q1, :, :], xhl[:, (k + 3) % 4, :, 0:D],
                                      ALU.subtract).then_inc(s_xn_lo, 1)
            phase_a(dve, slot)

            c = Chain(dve, s_tab_chain, 0, 33)
            c(dve.tensor_copy(seen_b[:, :], seen[:, :]))
            dve.wait_ge(s_cnt_ps, 1)
            dve.memset(t0[:, 0:1], 0.0)
            dve.tensor_copy(tabs[:, 2 * NT:], ps[0:1, 7, 0:E])
            c(dve.tensor_scalar(til_i[:, :], ps[:, 7, 0:E], TP - 1.0, None, ALU.add))
            c(dve.tensor_scalar(til_i[:, :], til_i[:, :], TP.bit_length() - 1, None, ALU.logical_shift_right))
            c(dve.tensor_copy(til[:, :], til_i[:, :]))
            c(dve.tensor_tensor_scan(t0[:, 1:], til[:, :], zero8[:, :], 0.0, ALU.add, ALU.add))
            c(dve.tensor_scalar(jump[:, :], til[:, :], -float(TP), float(CAP), ALU.mult, ALU.add))
            c(dve.memset(ef[:, :], 0.0))
            c(dve.tensor_scalar(rf[:, :], tile_no[:, :], float(TP), None, ALU.mult))
            for e in range(1, E):
                c(dve.tensor_scalar(past[:, :], tile_no[:, :], t0[:, e:e + 1], None, ALU.is_ge))
                c(dve.tensor_tensor(ef[:, :], ef[:, :], past[:, :], ALU.add))
                c(dve.scalar_tensor_tensor(rf[:, :], past[:, :], jump[:, e - 1:e], rf[:, :], ALU.mult, ALU.add))
            c(dve.tensor_scalar(past[:, :], tile_no[:, :], t0[:, E:E + 1], None, ALU.is_lt))
            c(dve.scalar_tensor_tensor(rf[:, :], rf[:, :], -float(E * CAP), past[:, :], ALU.add, ALU.mult))
            c(dve.tensor_scalar(tabs[:, 0:NT], rf[0:1, :], float(E * CAP), None, ALU.add))
            c(dve.tensor_scalar(code[:, :], ef[:, :], -1.0, float(E), ALU.mult, ALU.add))
            c.end()
            dve.tensor_copy(tabs[:, NT:2 * NT], ef[0:1, :]).then_inc(s_tab, 1)

            def slot_b(s, k):
                t, q, kr = s + 1, (k + 1) % 2, (k + 1) % RB
                if tile(t):
                    meta_in = row_in[:, kr, :, D:ROW].bitcast(F32)
                    dve.wait_ge(s_rT_ps, t + 1)
                    if since(t, RB):
                        dve.wait_ge(s_y_out[kr % YB], (t - kr) * (16 * TC // YB) + (kr // YB + 1 - RB // YB) * 16 * TC)
                    dve.nop(nofuse=True)
                    dve.tensor_scalar(is_first[:, :], meta_in[:, :, 1], code[:, bass.ds(t, 1)], None,
                                      ALU.is_equal).then_inc(s_sel, 1)
                    dve.wait_ge(s_sel, 3 * t + 1)
                    dve.tensor_tensor(y_idx[:, kr, :], meta_in[:, :, 0], is_first[:, :], ALU.subtract)
                    dve.tensor_tensor(w_sel[:, kr, :], meta_in[:, :, 2], is_first[:, :], ALU.mult).then_inc(s_sel, 1)
                    dve.wait_ge(s_sel, 3 * t + 2)
                    dve.tensor_tensor(w_sel[:, kr, :], w_sel[:, kr, :], meta_in[:, :, 3], ALU.add).then_inc(s_sel, 1)
                if tile(t):
                    if since(t, 2):
                        dve.wait_ge(s_down_ps, t - 1)
                    for half in range(2):
                        v = slice(half * HC // 2, (half + 1) * HC // 2)
                        dve.wait_ge(s_gelu, 2 * t + (half + 1))
                        dve.tensor_copy(hid_h(q)[:, v, :], hid(q)[:, v, :]).then_inc(s_hid_hi, 1)
                        dve.wait_ge(s_hid_hi, 2 * t + (half + 1))
                        dve.tensor_tensor(hid_l(q)[:, v, :], hid(q)[:, v, :], hid_h(q)[:, v, :],
                                          ALU.subtract).then_inc(s_hid_lo, 1)
            phase_b(dve, slot_b)

            with dve.Fori(0, B // CB // 2) as i:
                for q in range(2):
                    v = bass.ds(i * 2 * CB + q * CB, CB)
                    dve.wait_ge(s_y_in[q], i * 16 + 16)
                    dve.tensor_tensor(x1[:, v, :], x1[:, v, :], y_in(q)[:, :, 0:D], ALU.add).then_inc(s_c_half, 1)
                    dve.wait_ge(s_c_half, i * 2 + (q + 1))
                    dve.scalar_tensor_tensor(x1[:, v, :], x1[:, v, :], -1.0, y_in(q)[:, :, D:2 * D],
                                             ALU.add, ALU.add).then_inc(s_c_sum, 1)

        @block.tensor
        def _(pe):
            pe.wait_ge(s_const, 16)
            pe.wait_ge(s_w_rows, 16 * 9)
            pe.transpose(ps[:, 0, 0:50], small_rows[0:50, :], ident[0:50, 0:50]).then_inc(s_cols_T, 1)
            pe.transpose(ps[:, 1, 0:128], w_gnn[:, :], ident[:, :]).then_inc(s_wT_T, 1)
            pe.wait_ge(s_cols, 1)
            pe.wait_ge(s_wT, 1)
            pe.matmul(ps[:, 2, 0:2], w_gnnT[:, :], cols[:, 48:50], start=True, stop=True)
            pe.matmul(ps[:, 2, 2:2 + E], ones_row[:, :], br_row[:, :], start=True, stop=True).then_inc(s_wa_mm, 1)
            pe.wait_ge(s_reps, 1)

            def transposes(dst, src, q):
                for b in range(GB):
                    last = pe.transpose(dst[:, b, :], src[:, q, b, :], ident[:, :])
                return last

            def slot(s, k, j):
                if isinstance(s, int) and 0 <= s + 3 < E:
                    e = s + 3
                    pe.wait_ge(s_w_staged, 16 * (2 * e + 1))
                    for c in range(HC):
                        last = pe.matmul(ps[:, 7, e * HC + c:e * HC + c + 1], w_stage[:, 0, c * 128:(c + 1) * 128],
                                         cols[:, 40 + e:41 + e], start=True, stop=True)
                    last.then_inc(s_b1_mm, 1)
                g, q = s + 2, k % 2
                if group(g):
                    pe.wait_ge(s_hT, g + 1)
                    if since(g, 1):
                        pe.wait_ge(s_wh, g)
                    for b in range(GB):
                        last = pe.matmul(ps_wh[:, b, :], hT[:, q, b, :], w_gnn[:, :], start=True, stop=True)
                    last.then_inc(s_wh_ps, 1)
                    if since(g, 1):
                        pe.wait_ge(s_leaky, g)
                    pe.matmul(ps_s, ident_b[:, :], mask_b[:, :].unsqueeze(1).to_broadcast([128, GB, 128]),
                              start=True, stop=False)
                    pe.matmul(ps_s, wa2_rep[:, :], hT[:, q, :, :], start=False, stop=False)
                    for b in range(GB):
                        last = pe.matmul(ps_s[:, b, :], hT[:, q, b, :], wa1_rep[:, :], start=False, stop=b == GB - 1)
                    last.then_inc(s_s_ps, 1)
                g, q = s + 1, (k + 1) % 2
                if group(g):
                    pe.wait_ge(s_p, g + 1)
                    if since(g, 1):
                        pe.wait_ge(s_pT, g)
                    transposes(ps_pT, p, q).then_inc(s_pT_ps, 1)
                g, q = s + 3, (k + 3) % 2
                if group(g):
                    pe.wait_ge(s_h, g + 1)
                    if since(g, 1):
                        pe.wait_ge(s_hT, g)
                    transposes(ps_hT, h, q).then_inc(s_hT_ps, 1)
                g, q = s + 1, (k + 1) % 2
                if group(g):
                    pe.wait_ge(s_pT, g + 1)
                    pe.wait_ge(s_wh, g + 1)
                    if since(g, 1):
                        pe.wait_ge(s_hp, g)
                    for b in range(GB):
                        last = pe.matmul(ps_att[:, b, :], pT[:, q, b, :], wh[:, q, b, :], start=True, stop=True)
                    last.then_inc(s_att_ps, 1)
                if routes(s, k):
                    pe.wait_ge(s_seen, j + 1)
                    pe.wait_ge(s_both, j + 1)
                    pe.wait_ge(s_b1c, 1)
                    if not (isinstance(j, int) and j == 0):
                        if since(j, 1):
                            pe.wait_ge(s_route, j * ROUTE)
                    pe.matmul(ps_r, ones_b[:, :], seen_b[:, :].unsqueeze(1).to_broadcast([128, BLK, E]),
                              start=True, stop=False)
                    for b in range(BLK - 1):
                        pe.matmul(ps_r[:, b + 1:BLK, :], ones_b[:, :],
                                  both[:, b:b + 1, :].to_broadcast([128, BLK - 1 - b, E]),
                                  start=False, stop=False)
                    last = pe.matmul(ps_r, tri_b[:, :], both[:, :, :], start=False, stop=True)
                    last.then_inc(s_rank_ps, 1)
                g, q = s - 1, (k - 1) % 2
                if group(g):
                    pe.wait_ge(s_xn, g + 1)
                    if since(g, 1):
                        pe.wait_ge(s_xT, g)
                    transposes(ps_xT, xn, q).then_inc(s_xT_ps, 1)
                    pe.wait_ge(s_xT, g + 1)
                    if since(g, 1):
                        pe.wait_ge(s_l, g)
                    for b in range(GB):
                        last = pe.matmul(ps_l[:, b, :], xnT[:, q, b, :], wr[:, :], start=True, stop=True)
                    last.then_inc(s_l_ps, 1)
            phase_a(pe, slot)
            pe.wait_ge(s_tab_chain, 1)
            pe.matmul(ps[:, 7, 0:E], ones_b[:, :], seen_b[:, :], start=True, stop=True).then_inc(s_cnt_ps, 1)
            pe.wait_ge(s_b2_moved, 32)
            pe.wait_ge(s_tab, 1)

            expert_of = {}

            def expert(t, k):
                e = expert_of.get(k)
                if e is None:
                    e = pe.value_load(tabs[0:1, bass.ds(t + NT, 1)], min_val=0, max_val=E - 1)
                expert_of.clear()
                expert_of[k] = e
                return e

            def slot_b(s, k):
                t, q, kr = s + 2, k % 2, (k + 2) % RB
                if tile(t):
                    pe.wait_ge(s_rows_in[kr], (t - kr) * (16 // RB) + 16)
                    if since(t, 2):
                        pe.wait_ge(s_rT, t - 1)
                    for part in range(2):
                        for c in range(TC):
                            n = part * TC + c
                            last = pe.transpose(ps_rT(q)[:, n * 128:(n + 1) * 128],
                                                row_in[:, kr, c, part * (D // 2):(part + 1) * (D // 2)].bitcast(F16), ident16[:, :])
                    last.then_inc(s_rT_ps, 1)
                t, q = s + 1, (k + 1) % 2
                if tile(t):
                    e = expert(t, (k + 1) % RB)
                    pe.wait_ge(s_rT, t + 1)
                    if since(t, 1):
                        pe.wait_ge(s_gelu, 2 * t)
                    for c in range(HC):
                        v = bass.ds(e * H + c * 128, 128)
                        pe.matmul(ps_up[:, c, :], w1h[:, v], rT[:, q, 0:TP], start=True, stop=False)
                        pe.matmul(ps_up[:, c, :], w1h[:, v], rT[:, q, TP:], start=False, stop=False)
                        last = pe.matmul(ps_up[:, c, :], w1l[:, v], rT[:, q, 0:TP], start=False, stop=True)
                        if c % (HC // 2) == HC // 2 - 1:
                            last.then_inc(s_up_ps, 1)
                t, q = s, k % 2
                if tile(t):
                    e = expert(t, k)
                    pe.wait_ge(s_hid_lo, 2 * t + 2)
                    if since(t, 2):
                        pe.wait_ge(s_yw, t - 1)
                    pe.matmul(ps_y(q), ones2[:, :], b2_hl[:, bass.ds(e * D, D)].unsqueeze(1).to_broadcast([2, TC, D]),
                              start=True, stop=False)
                    for c in range(HC):
                        v = bass.ds(e * H + c * D, D)
                        for part, w in ((hid_h, w2h), (hid_l, w2h), (hid_h, w2l)):
                            for n in range(TC):
                                last = pe.matmul(ps_y(q)[:, n, :], part(q)[:, c, n * 128:(n + 1) * 128], w[:, v],
                                                 start=False, stop=c == HC - 1 and w is w2l and n == TC - 1)
                    last.then_inc(s_down_ps, 1)
            phase_b(pe, slot_b)


_INS = ['x', 'adj', 'L0_gnn_W', 'L0_gnn_a', 'L0_ffn_Wr', 'L0_ffn_br', 'L0_ffn_ln_g', 'L0_ffn_ln_b', 'L0_ffn_W1',
        'L0_ffn_b1', 'L0_ffn_W2', 'L0_ffn_b2']
_OUTS = [((B, N, D), 'float32')]


def kernel(**inputs):
    import numpy as _np
    import concourse.bacc as _bacc
    from concourse import mybir as _mybir
    from concourse.bass_utils import run_bass_kernel_spmd as _run

    nc = _bacc.Bacc("TRN2", target_bir_lowering=False, num_devices=1)
    arrays, args = {}, []
    for name in _INS:
        v = _np.ascontiguousarray(inputs[name])
        arrays[f"in_{name}_dram"] = v
        args.append(nc.dram_tensor(f"in_{name}_dram", v.shape, _mybir.dt.from_np(v.dtype), kind="ExternalInput").ap())
    for i, (shape, dtype) in enumerate(_OUTS):
        dt = _mybir.dt.from_np(_np.dtype(dtype))
        args.append(nc.dram_tensor(f"out_{i}_dram", shape, dt, kind="ExternalOutput").ap())
    program(nc, *args)
    r = _run(nc, [arrays], core_ids=[0])
    got = tuple(r.results[0][f"out_{i}_dram"] for i in range(len(_OUTS)))
    return got[0]
```

```python
import concourse.bass as bass
from concourse import mybir
from contextlib import ExitStack

F32 = mybir.dt.float32
F16 = mybir.dt.float16
BF16 = mybir.dt.bfloat16
I32 = mybir.dt.int32
ALU = mybir.AluOpType
ACT = mybir.ActivationFunctionType
AXX = mybir.AxisListType.X

B, N, D = 128, 128, 128
E, H = 8, 512
HC = H // 128
GB = 4
NG = B // GB
CB = 8
BLK = 4 * GB
PAIRS = 2 * B * N
TP = 512
TC = TP // 128
NT = (PAIRS + E * (TP - 1)) // TP
RB, YB = 4, 2
CAP = B * N + TP
META = 4
ROW = D + META
EPS = 1e-5
ROUTE = 19
SLOPE = 0.2
GUESS = float(0x5f3759df)
NEG = -1e30
WS = 64.0


def program(nc, x, adj, W, a, Wr, br, ln_g, ln_b, W1, b1, W2, b2, out):
    ctx = ExitStack()
    with ctx:
        def sb(name, shape, dt=F32):
            return ctx.enter_context(nc.sbuf_tensor(name, shape, dt))

        def sem(name):
            return ctx.enter_context(nc.semaphore(name))

        rows_d = nc.dram_tensor("rows_d", [E * CAP + TP, ROW], I32).ap()
        y_d = nc.dram_tensor("y_d", [PAIRS, D], F32).ap()

        ps = ctx.enter_context(nc.psum_tensor("ps", [128, 8, 512], F32))

        def bank(n):
            return ps[:, n, :].rearrange("p (b d) -> p b d", b=GB)
        ps_hT, ps_wh, ps_s, ps_pT, ps_att, ps_xT = (bank(n) for n in range(6))
        ps_l = ps[:, 6, 0:GB * E].rearrange("p (b e) -> p b e", e=E)
        ps_r = ps[:, 7, 0:BLK * E].rearrange("p (b e) -> p b e", e=E)

        ident = sb("ident", [128, 128])
        ident16 = sb("ident16", [128, 128], F16)
        ones_b = sb("ones_b", [128, 128], BF16)
        tri_b = sb("tri_b", [128, 128], BF16)
        ones2 = sb("ones2", [2, 128], F16)
        rev = sb("rev", [128, E])
        ecap = sb("ecap", [128, E])
        ids = sb("ids", [128, B], I32)
        pad = sb("pad", [128, ROW], I32)
        tile_no = sb("tile_no", [128, NT])
        iota_i = sb("iota_i", [128, 2 * E + NT], I32)
        zero8 = sb("zero8", [128, E])
        adj_i = sb("adj_i", [128, 128], I32)
        mask_bias = sb("mask_bias", [128, 128])
        mask_b = sb("mask_b", [128, 128], BF16)
        ident_b = sb("ident_b", [128, 128], BF16)
        w_gnn = sb("w_gnn", [128, 128])
        w_gnnT = sb("w_gnnT", [128, 128])
        small_rows = sb("small_rows", [64, 128])
        cols = sb("cols", [128, 64])
        wa = sb("wa", [128, 2])
        wa1_rep = sb("wa1_rep", [128, 128])
        wa2_rep = sb("wa2_rep", [128, 128])
        wr = sb("wr", [128, E])
        br_row = sb("br_row", [1, E])
        br_rep = sb("br_rep", [128, E])
        ones_row = sb("ones_row", [1, 128])
        g_ws = sb("g_ws", [128, E])
        w_stage = sb("w_stage", [128, 4, H])
        w1h = sb("w1h", [128, E * H], F16)
        w1l = sb("w1l", [128, E * H], F16)
        w2h = sb("w2h", [128, E * H], F16)
        w2l = sb("w2l", [128, E * H], F16)
        b1c = sb("b1c", [128, E * HC])
        b2_f = sb("b2_f", [1, E * D])
        b2_h = sb("b2_h", [1, E * D], F16)
        b2_l = sb("b2_l", [1, E * D], F16)
        b2_hl = sb("b2_hl", [2, E * D], F16)
        arena = sb("arena", [128, 10 * 2 * GB * 128])
        h, hT, wh, e_sc, p, pT, hp, ex, xn, xnT = (
            arena[:, n * 2 * GB * 128:(n + 1) * 2 * GB * 128].rearrange("p (a b d) -> p a b d", a=2, b=GB)
            for n in range(10))
        x1 = sb("x1", [128, B, D])
        st1 = sb("st1", [128, 2, GB, 6])
        mv1 = sb("mv1", [128, 2, GB, 2])
        nbias1 = sb("nbias1", [128, 2, GB])
        nmx = sb("nmx", [128, 2, GB])
        sm = sb("sm", [128, 2, GB])
        rsm = sb("rsm", [128, 2, GB])
        st2 = sb("st2", [128, 2, GB, 6])
        mv2 = sb("mv2", [128, 2, GB, 2])
        veps = sb("veps", [128, 2, 3 * GB])
        half_bits = sb("half_bits", [128, 3 * GB], I32)
        guess = sb("guess", [128, 3 * GB])
        root = sb("root", [128, 3 * GB])
        ratio = sb("ratio", [128, 3 * GB])
        rinv = sb("rinv", [128, 2, 3 * GB])
        rec2 = sb("rec2", [128, GB])
        rtot = sb("rtot", [128, 2, GB])
        nbias2 = sb("nbias2", [128, 2, GB])
        unsc = sb("unsc", [128, 2, GB])
        lg = sb("lg", [128, BLK, E])
        lg2 = sb("lg2", [128, BLK, E])
        eq = sb("eq", [128, BLK, E])
        top1 = sb("top1", [128, BLK])
        top2 = sb("top2", [128, BLK])
        pick = sb("pick", [128, 2, BLK])
        oh1 = sb("oh1", [128, BLK, E])
        oh2 = sb("oh2", [128, BLK, E])
        both = sb("both", [128, BLK, E], BF16)
        blk_sum = sb("blk_sum", [128, E])
        seen = sb("seen", [128, E])
        seen_b = sb("seen_b", [128, E], BF16)
        gap = sb("gap", [128, BLK])
        egap = sb("egap", [128, BLK])
        den = sb("den", [128, BLK])
        rk = sb("rk", [128, BLK, E])
        pos = sb("pos", [128, 2, BLK])
        meta = sb("meta", [128, BLK, META])
        row_out = sb("row_out", [128, 4, GB, ROW], I32)
        idx = sb("idx", [128, 4, 2 * GB], I32)
        til_i = sb("til_i", [128, E], I32)
        til = sb("til", [128, E])
        t0 = sb("t0", [128, E + 1])
        jump = sb("jump", [128, E])
        past = sb("past", [128, NT])
        rf = sb("rf", [128, NT])
        ef = sb("ef", [128, NT])
        code = sb("code", [128, NT])
        tabs = sb("tabs", [1, 2 * NT + E], I32)
        row_in = sb("row_in", [128, RB, TC, ROW], I32)
        rT = sb("rT", [128, 2, 2 * TP], F16)
        yw = sb("yw", [128, YB, TC, D])
        is_first = sb("is_first", [128, TC])
        w_sel = sb("w_sel", [128, RB, TC])
        y_idx = sb("y_idx", [128, RB, TC], I32)

        s_const = sem("s_const")
        s_w_rows = sem("s_w_rows")
        s_cols_T = sem("s_cols_T")
        s_cols = sem("s_cols")
        s_wT_T = sem("s_wT_T")
        s_wT = sem("s_wT")
        s_wa_mm = sem("s_wa_mm")
        s_wa = sem("s_wa")
        s_reps = sem("s_reps")
        s_prep = sem("s_prep")
        s_w_staged = sem("s_w_staged")
        s_w_hi = sem("s_w_hi")
        s_w_lo = sem("s_w_lo")
        s_b1_mm = sem("s_b1_mm")
        s_b1c = sem("s_b1c")
        s_b2_parts = sem("s_b2_parts")
        s_b2_moved = sem("s_b2_moved")
        s_x_in = sem("s_x_in")
        s_veps_set = sem("s_veps_set")
        s_stats1 = sem("s_stats1")
        s_aggr1 = sem("s_aggr1")
        s_veps1 = sem("s_veps1")
        s_root = sem("s_root")
        s_sel = sem("s_sel")
        s_nbias1 = sem("s_nbias1")
        s_h = sem("s_h")
        s_hT_ps = sem("s_hT_ps")
        s_hT = sem("s_hT")
        s_wh_ps = sem("s_wh_ps")
        s_wh = sem("s_wh")
        s_s_ps = sem("s_s_ps")
        s_relu = sem("s_relu")
        s_leaky = sem("s_leaky")
        s_nmx = sem("s_nmx")
        s_p = sem("s_p")
        s_pT_ps = sem("s_pT_ps")
        s_pT = sem("s_pT")
        s_att_ps = sem("s_att_ps")
        s_rsm = sem("s_rsm")
        s_rtot = sem("s_rtot")
        s_hp = sem("s_hp")
        s_ex = sem("s_ex")
        s_elu = sem("s_elu")
        s_x1 = sem("s_x1")
        s_stats2 = sem("s_stats2")
        s_aggr2 = sem("s_aggr2")
        s_veps2 = sem("s_veps2")
        s_rec2 = sem("s_rec2")
        s_vqe = sem("s_vqe")
        s_vq = sem("s_vq")
        s_scales = sem("s_scales")
        s_xn = sem("s_xn")
        s_xn_hi = sem("s_xn_hi")
        s_xn_lo = sem("s_xn_lo")
        s_xT_ps = sem("s_xT_ps")
        s_xT = sem("s_xT")
        s_l_ps = sem("s_l_ps")
        s_l = sem("s_l")
        s_route = sem("s_route")
        s_gap = sem("s_gap")
        s_egap = sem("s_egap")
        s_both = sem("s_both")
        s_seen = sem("s_seen")
        s_rank_ps = sem("s_rank_ps")
        s_pos = sem("s_pos")
        s_rows = sem("s_rows")
        s_cnt_ps = sem("s_cnt_ps")
        s_tab_chain = sem("s_tab_chain")
        s_tab = sem("s_tab")
        s_pads = sem("s_pads")
        s_rT_ps = sem("s_rT_ps")
        s_rT = sem("s_rT")
        s_up_ps = sem("s_up_ps")
        s_gelu = sem("s_gelu")
        s_hid_hi = sem("s_hid_hi")
        s_hid_lo = sem("s_hid_lo")
        s_down_ps = sem("s_down_ps")
        s_yw = sem("s_yw")
        s_c_half = sem("s_c_half")
        s_c_sum = sem("s_c_sum")
        s_stored = sem("s_stored")
        s_scat = [sem(f"s_scat{n}") for n in range(4)]
        s_rows_in = [sem(f"s_rows_in{n}") for n in range(RB)]
        s_y_out = [sem(f"s_y_out{n}") for n in range(YB)]
        s_y_in = [sem(f"s_y_in{n}") for n in range(2)]

        def since(n, first):
            return not isinstance(n, int) or n >= first

        class Chain:
            def __init__(self, eng, sem, base, steps):
                self.eng, self.sem, self.base, self.steps, self.n = eng, sem, base, steps, 0

            def __call__(self, ins):
                self.step(ins)
                self.wait()

            def step(self, ins):
                self.n += 1
                ins.then_inc(self.sem, 1)

            def wait(self):
                self.eng.wait_ge(self.sem, self.base + self.n)

            def end(self):
                assert self.n == self.steps, self.n

        def group(g):
            return not isinstance(g, int) or 0 <= g < NG

        def of(g, b=None):
            return bass.ds(g * GB, GB) if b is None else bass.ds(g * GB + b, 1)

        def x1_of(g, b):
            return x1[:, of(g, b), :].rearrange("p a d -> p (a d)")

        LOOP_A = 8
        TURNS_A = (NG - 4 - LOOP_A) // 4

        def phase_a(eng, slot):
            for s in range(-4, LOOP_A):
                slot(s, s % 4, (s - 5) // 4)
            with eng.Fori(0, TURNS_A) as i:
                for k in range(4):
                    slot(i * 4 + (LOOP_A + k), (LOOP_A + k) % 4, i + (LOOP_A - 4) // 4)
            for s in range(LOOP_A + 4 * TURNS_A, NG + 5):
                slot(s, s % 4, (s - 5) // 4)

        def routes(s, k):
            return k == 1 and not (isinstance(s, int) and s < 5)

        FIRST_B = RB
        TURNS_B = (NT - FIRST_B - 2) // RB

        def phase_b(eng, slot):
            for s in range(-2, FIRST_B):
                slot(s, s % RB)
            with eng.Fori(0, TURNS_B) as i:
                for k in range(RB):
                    slot(i * RB + (FIRST_B + k), k)
            for s in range(FIRST_B + RB * TURNS_B, NT):
                slot(s, s % RB)

        def tile(t):
            return not isinstance(t, int) or 0 <= t < NT

        ps_rT = ps[:, 0:2, :]
        ps_up = ps[:, 2:6, :]

        def ps_y(q):
            return ps[:, 6 + q, :].rearrange("p (s d) -> p s d", s=TC)

        def hid(q):
            return arena[:, q * HC * TP:(q + 1) * HC * TP].rearrange("p (c t) -> p c t", c=HC)

        def part_of(n):
            first = 2 * HC * TP + n * HC * TP // 2
            return arena[:, first:first + HC * TP // 2].bitcast(F16).rearrange("p (c t) -> p c t", c=HC)

        def hid_h(q):
            return part_of(2 * q)

        def hid_l(q):
            return part_of(2 * q + 1)


        def y_in(q):
            return (w1h, w1l)[q][:, :].bitcast(F32).rearrange("p (b d) -> p b d", b=CB)

        block = ctx.enter_context(nc.Block())

        @block.sync
        def _(sp):
            xv = x.rearrange("b n d -> n b d")

            def load_x(i):
                if since(i, 1):
                    sp.wait_ge(s_x_in, i * 16)
                v = bass.ds(i * CB, CB)
                sp.dma_start(x1[:, v, :], xv[:, v, :]).then_inc(s_x_in, 16)

            load_x(0)
            load_x(1)
            for dst, src in [(adj_i[:, :], adj), (w_gnn[:, :], W), (wr[:, :], Wr),
                             (br_row[:, :], br.rearrange("(o e) -> o e", o=1)),
                             (small_rows[0:32, :], b1.rearrange("e (c p) -> (e c) p", p=128)),
                             (small_rows[32:40, :], ln_g), (small_rows[40:48, :], ln_b),
                             (small_rows[48:50, :], a.rearrange("(r p) o -> r (p o)", r=2)),
                             (b2_f[:, :], b2.rearrange("(o e) d -> o (e d)", o=1))]:
                sp.dma_start(dst, src).then_inc(s_w_rows, 16)
            for n in range(2 * E):
                if n >= 1:
                    sp.wait_ge(s_w_staged, 16 * n)
                if n >= 4:
                    sp.wait_ge(s_w_lo, n - 3)
                if n >= 4 and n % 2 == 0:
                    sp.wait_ge(s_b1_mm, n // 2 - 1)
                if n % 2 == 0:
                    src, dst = W1[n // 2], w_stage[:, n % 4, :]
                else:
                    src = W2[n // 2].rearrange("(c p) d -> p c d", p=128)
                    dst = w_stage[:, n % 4, :].rearrange("p (c d) -> p c d", c=HC)
                sp.dma_start(dst, src).then_inc(s_w_staged, 16)
                if n in (5, 9):
                    load_x(2 if n == 5 else 3)
            sp.wait_ge(s_b2_parts, 2)
            sp.dma_start(b2_hl[0:1, :], b2_h[:, :]).then_inc(s_b2_moved, 16)
            sp.dma_start(b2_hl[1:2, :], b2_l[:, :]).then_inc(s_b2_moved, 16)
            with sp.Fori(4, B // CB) as i:
                load_x(i)

            sp.wait_ge(s_tab, 1)
            no_pair = pad[:, :].rearrange("p (c r) -> p c r", c=1).to_broadcast([128, TP // 128, ROW])
            for e in range(E):
                n_e = sp.value_load(tabs[0:1, 2 * NT + e:2 * NT + e + 1], min_val=0, max_val=B * N)
                sp.dma_start(rows_d[bass.ds(n_e + e * CAP, TP), :].rearrange("(c p) r -> p c r", p=128),
                             no_pair).then_inc(s_pads, 16)
            sp.dma_start(rows_d[E * CAP:E * CAP + TP, :].rearrange("(c p) r -> p c r", p=128),
                         no_pair).then_inc(s_pads, 16)
            sp.wait_ge(s_pads, 16 * (E + 1))
            for q in range(4):
                sp.wait_ge(s_scat[q], 128 * (NG // 4))

            def load_rows(t, k):
                r = sp.value_load(tabs[0:1, bass.ds(t, 1)], min_val=0, max_val=E * CAP)
                sp.dma_start(row_in[:, k, :, :], rows_d[bass.ds(r, TP), :].rearrange("(c p) r -> p c r", p=128))\
                    .then_inc(s_rows_in[k], 16)

            for k in range(RB):
                load_rows(k, k)

            def reload_rows(i, k):
                sp.wait_ge(s_sel, i * (3 * RB) + 3 * (k - RB + 1))
                load_rows(i * RB + k, k)

            with sp.Fori(1, NT // RB) as i:
                for k in range(RB):
                    reload_rows(i, k)
            for k in range(NT % RB):
                reload_rows(NT // RB, k)

            for q in range(YB):
                sp.wait_ge(s_y_out[q], 16 * TC * ((NT - q + YB - 1) // YB))
            yv = y_d.rearrange("(b n k) d -> n b (k d)", n=N, k=2)
            ov = out.rearrange("b n d -> n b d")

            def load_y(c, q):
                sp.dma_start(y_in(q), yv[:, bass.ds(c * CB, CB), :]).then_inc(s_y_in[q], 16)

            def store(c):
                sp.wait_ge(s_c_sum, c + 1)
                v = bass.ds(c * CB, CB)
                sp.dma_start(ov[:, v, :], x1[:, v, :]).then_inc(s_stored, 16)

            for q in range(2):
                load_y(q, q)
            with sp.Fori(0, B // CB // 2 - 1) as i:
                for q in range(2):
                    store(i * 2 + q)
                    load_y(i * 2 + (2 + q), q)
            for q in range(2):
                store(B // CB - 2 + q)
            sp.wait_ge(s_stored, 16 * (B // CB))

        @block.gpsimd
        def _(pool):
            for t, v in ((ident, 0.0), (tri_b, 1.0), (ones_b, 1.0), (ones2, 1.0), (ones_row, 1.0),
                         (seen, 0.0), (zero8, 0.0)):
                pool.memset(t[:, :], v).then_inc(s_const, 1)
            pool.memset(pad[:, 0:D], 0).then_inc(s_const, 1)
            pool.memset(pad[:, D:D + 1].bitcast(F32), PAIRS + 1.0).then_inc(s_const, 1)
            pool.memset(pad[:, D + 1:ROW], 0).then_inc(s_const, 1)
            pool.iota(ids[:, :], pattern=[[2 * N, B]], base=1, channel_multiplier=2).then_inc(s_const, 1)
            pool.iota(iota_i[:, 0:E], pattern=[[-1, E]], base=E, channel_multiplier=0).then_inc(s_const, 1)
            pool.iota(iota_i[:, E:2 * E], pattern=[[CAP, E]], base=0, channel_multiplier=0).then_inc(s_const, 1)
            pool.iota(iota_i[:, 2 * E:], pattern=[[1, NT]], base=0, channel_multiplier=0).then_inc(s_const, 1)
            pool.wait_ge(s_const, 14)
            pool.affine_select(out=ident[:, :], in_=ident[:, :], compare_op=ALU.not_equal, fill=1.0, base=0,
                               pattern=[[-1, 128]], channel_multiplier=1).then_inc(s_const, 1)
            pool.affine_select(out=tri_b[:, :], in_=tri_b[:, :], compare_op=ALU.is_gt, fill=0.0, base=0,
                               pattern=[[1, 128]], channel_multiplier=-1).then_inc(s_const, 1)

            def slot(s, k, j):
                g = s - 5
                if group(g):
                    pool.wait_ge(s_xn_lo, g + 1)
                    pool.wait_ge(s_rows, g + 1)
                    pool.nop(nofuse=True)
                    for n in range(2 * GB):
                        pool.indirect_dma_start(
                            rows_d[:, :], bass.IndirectOffsetOnAxis(ap=idx[:, (k + 3) % 4, n:n + 1], axis=0),
                            row_out[:, (k + 3) % 4, n % GB, :], None).then_inc(s_scat[(k + 3) % 4], 16)
            phase_a(pool, slot)

            def slot_b(s, k):
                if tile(s) and not (isinstance(s, int) and s < 0):
                    pool.wait_ge(s_yw, s + 1)
                    pool.nop(nofuse=True)
                    for c in range(TC):
                        pool.indirect_dma_start(
                            y_d[:, :],
                            bass.IndirectOffsetOnAxis(ap=y_idx[:, k, c:c + 1], axis=0),
                            yw[:, k % YB, c, :], None, bounds_check=PAIRS - 1,
                            oob_is_err=False).then_inc(s_y_out[k % YB], 16)
            phase_b(pool, slot_b)

        @block.scalar
        def _(act):
            def slot(s, k, j):
                g, q = s + 1, (k + 1) % 2
                if group(g):
                    act.wait_ge(s_nmx, g + 1)
                    for b in range(GB):
                        last = act.activation(p[:, q, b, :], p[:, q, b, :], ACT.Exp, bias=nmx[:, q, b:b + 1],
                                              accum_out=sm[:, q, b:b + 1])
                    last.then_inc(s_p, 1)
                g, q = s, k % 2
                if group(g):
                    act.wait_ge(s_hp, g + 1)
                    act.activation(ex[:, q, :, :], hp[:, q, :, :], ACT.Exp).then_inc(s_ex, 1)
                g, q = s - 2, k % 2
                if group(g):
                    act.wait_ge(s_xT_ps, g + 1)
                    if since(g, 2):
                        act.wait_ge(s_l_ps, g - 1)
                    act.copy(xnT[:, q, :, :], ps_xT).then_inc(s_xT, 1)
                g, q = s + 2, k % 2
                if group(g):
                    act.wait_ge(s_wh_ps, g + 1)
                    if since(g, 2):
                        act.wait_ge(s_att_ps, g - 1)
                    act.copy(wh[:, q, :, :], ps_wh).then_inc(s_wh, 1)
                if isinstance(s, int) and 0 <= s + 3 < E:
                    e = s + 3
                    act.wait_ge(s_cols, 2)
                    act.wait_ge(s_w_staged, 16 * (2 * e + 1))
                    act.activation(w1h[:, e * H:(e + 1) * H], w_stage[:, e % 2 * 2, :], ACT.Copy,
                                   scale=g_ws[:, e:e + 1]).then_inc(s_w_hi, 1)
                    act.wait_ge(s_w_staged, 16 * (2 * e + 2))
                    act.activation(w2h[:, e * H:(e + 1) * H], w_stage[:, e % 2 * 2 + 1, :], ACT.Copy, scale=WS).then_inc(s_w_hi, 1)
                g, q = s + 2, k % 2
                if group(g):
                    act.wait_ge(s_s_ps, g + 1)
                    if since(g, 2):
                        act.wait_ge(s_leaky, g - 1)
                    act.activation(e_sc[:, q, :, :], ps_s, ACT.Relu, scale=SLOPE - 1.0).then_inc(s_relu, 1)
                g, q = s + 1, (k + 1) % 2
                if group(g):
                    act.wait_ge(s_pT_ps, g + 1)
                    if since(g, 2):
                        act.wait_ge(s_att_ps, g - 1)
                    act.copy(pT[:, q, :, :], ps_pT).then_inc(s_pT, 1)
                g, q = s + 3, (k + 3) % 2
                if group(g):
                    act.wait_ge(s_nbias1, g + 1)
                    if since(g, 2):
                        act.wait_ge(s_hT_ps, g - 1)
                    act.nop(nofuse=True)
                    for b in range(GB):
                        last = act.activation(h[:, q, b, :], x1_of(g, b), ACT.Identity, bias=nbias1[:, q, b:b + 1],
                                              scale=rinv[:, q, b:b + 1])
                    last.then_inc(s_h, 1)
                g, q = s - 1, (k - 1) % 2
                if group(g):
                    act.wait_ge(s_scales, g + 1)
                    if since(g, 2):
                        act.wait_ge(s_xT_ps, g - 1)
                        act.wait_ge(s_xn_lo, g - 1)
                    act.nop(nofuse=True)
                    for b in range(GB):
                        last = act.activation(xn[:, q, b, :], x1_of(g, b), ACT.Identity, bias=nbias2[:, q, b:b + 1],
                                              scale=rtot[:, q, b:b + 1])
                    last.then_inc(s_xn, 1)
                g, q = s + 3, (k + 3) % 2
                if group(g):
                    act.wait_ge(s_hT_ps, g + 1)
                    if since(g, 2):
                        act.wait_ge(s_s_ps, g - 1)
                    act.copy(hT[:, q, :, :], ps_hT).then_inc(s_hT, 1)
                if routes(s, k):
                    act.wait_ge(s_gap, j + 1)
                    act.activation(egap[:, :], gap[:, :], ACT.Exp).then_inc(s_egap, 1)
            phase_a(act, slot)
            act.wait_ge(s_tab, 1)
            act.activation(egap[:, 0:1], egap[:, 0:1], ACT.Gelu)

            def slot_b(s, k):
                t, q = s + 2, k % 2
                if tile(t):
                    act.wait_ge(s_rT_ps, t + 1)
                    if since(t, 2):
                        act.wait_ge(s_up_ps, 2 * t - 2)
                    act.copy(rT[:, q, :], ps_rT.rearrange("p c t -> p (c t)")).then_inc(s_rT, 1)
                t, q = s + 1, (k + 1) % 2
                if tile(t):
                    e = act.value_load(tabs[0:1, bass.ds(t + NT, 1)], min_val=0, max_val=E - 1)
                    if since(t, 2):
                        act.wait_ge(s_hid_lo, 2 * t - 2)
                    for half in range(2):
                        act.wait_ge(s_up_ps, 2 * t + (half + 1))
                        act.nop(nofuse=True)
                        for c in range(half * HC // 2, (half + 1) * HC // 2):
                            last = act.activation(hid(q)[:, c, :], ps_up[:, c, :], ACT.Gelu,
                                                  bias=b1c[:, bass.ds(e * HC + c, 1)], scale=1.0 / WS)
                        last.then_inc(s_gelu, 1)
                t, q = s, k % 2
                if tile(t):
                    act.wait_ge(s_down_ps, t + 1)
                    act.wait_ge(s_sel, 3 * t + 3)
                    r = k % YB
                    if since(t, YB):
                        act.wait_ge(s_y_out[r], (t - r) * (16 * TC // YB))
                    for c in range(TC):
                        last = act.activation(yw[:, r, c, :], ps_y(q)[:, c, :], ACT.Copy,
                                              scale=w_sel[:, k, c:c + 1])
                    last.then_inc(s_yw, 1)
            phase_b(act, slot_b)

        @block.vector
        def _(dve):
            def spread(ap, shape, dim):
                return ap.unsqueeze(dim).to_broadcast(shape)

            dve.wait_ge(s_const, 16)
            dve.tensor_copy(ident16[:, :], ident[:, :])
            dve.tensor_copy(rev[:, :], iota_i[:, 0:E])
            dve.tensor_copy(ecap[:, :], iota_i[:, E:2 * E])
            dve.tensor_copy(tile_no[:, :], iota_i[:, 2 * E:]).then_inc(s_prep, 1)
            dve.wait_ge(s_w_rows, 16 * 9)
            prep = Chain(dve, s_prep, 1, 4)
            prep(dve.tensor_scalar(mask_bias[:, :], adj_i[:, :], 0.0, None, ALU.is_gt))
            prep(dve.tensor_tensor(mask_bias[:, :], mask_bias[:, :], ident[:, :], ALU.max))
            prep(dve.tensor_scalar(mask_bias[:, :], mask_bias[:, :], 1.0, -NEG, ALU.subtract, ALU.mult))
            dve.tensor_copy(ident_b[:, :], ident[:, :])
            prep(dve.tensor_copy(mask_b[:, :], mask_bias[:, :]))
            prep.end()
            dve.memset(veps[:, :, :], 1.0).then_inc(s_veps_set, 1)
            dve.wait_ge(s_veps_set, 1)
            dve.tensor_scalar(b2_h[:, :], b2_f[:, :], WS, None, ALU.mult).then_inc(s_b2_parts, 1)
            dve.wait_ge(s_b2_parts, 1)
            dve.scalar_tensor_tensor(b2_l[:, :], b2_f[:, :], WS, b2_h[:, :], ALU.mult, ALU.subtract).then_inc(s_b2_parts, 1)
            dve.wait_ge(s_cols_T, 1)
            dve.tensor_copy(cols[:, 0:50], ps[:, 0, 0:50]).then_inc(s_cols, 1)
            dve.wait_ge(s_cols, 1)
            dve.tensor_scalar(g_ws[:, :], cols[:, 32:40], WS, None, ALU.mult).then_inc(s_cols, 1)
            dve.wait_ge(s_wT_T, 1)
            dve.tensor_copy(w_gnnT[:, :], ps[:, 1, 0:128]).then_inc(s_wT, 1)
            dve.wait_ge(s_wa_mm, 1)
            dve.tensor_copy(br_rep[:, :], ps[:, 2, 2:2 + E])
            dve.tensor_copy(wa[:, :], ps[:, 2, 0:2]).then_inc(s_wa, 1)
            dve.wait_ge(s_wa, 1)
            dve.tensor_copy(wa1_rep[:, :], wa[:, 0:1].to_broadcast([128, 128]))
            dve.tensor_copy(wa2_rep[:, :], wa[:, 1:2].to_broadcast([128, 128])).then_inc(s_reps, 1)

            def stats(g, q, st, s_stats):
                dve.nop(nofuse=True)
                for b in range(GB):
                    last = dve.bn_stats(st[:, q, b, :], x1_of(g, b))
                last.then_inc(s_stats, 1)

            def mean_variance(g, q, st, mv, s_stats, s_aggr):
                dve.wait_ge(s_stats, g + 1)
                dve.nop(nofuse=True)
                for b in range(GB):
                    last = dve.bn_aggr(mv[:, q, b, :], st[:, q, b, :])
                last.then_inc(s_aggr, 1)

            ALLE = [128, BLK, E]

            def picks(j, c, aside):
                dve.wait_ge(s_l, j * 4 + 4)
                c(dve.tensor_tensor(lg[:, :, :], lg[:, :, :], spread(br_rep[:, :], ALLE, 1), ALU.add))
                for src, top, oh, n in ((lg, top1, oh1, 0), (lg2, top2, oh2, 1)):
                    c.step(dve.tensor_reduce(top[:, :], src[:, :, :], AXX, ALU.max))
                    if n == 0:
                        aside(0)
                        c.wait()
                    else:
                        c.wait()
                        dve.tensor_tensor(gap[:, :], top2[:, :], top1[:, :], ALU.subtract).then_inc(s_gap, 1)
                    c.step(dve.tensor_tensor(eq[:, :, :], src[:, :, :], spread(top[:, :], ALLE, 2), ALU.is_equal))
                    aside(4 * n + 1)
                    c.wait()
                    c.step(dve.tensor_tensor(eq[:, :, :], eq[:, :, :], spread(rev[:, :], ALLE, 1), ALU.mult))
                    aside(4 * n + 2)
                    c.wait()
                    c.step(dve.tensor_reduce(pick[:, n, :], eq[:, :, :], AXX, ALU.max))
                    aside(4 * n + 3)
                    c.wait()
                    c.step(dve.tensor_tensor(oh[:, :, :], spread(pick[:, n, :], ALLE, 2), spread(rev[:, :], ALLE, 1),
                                             ALU.is_equal))
                    if n == 0:
                        dve.tensor_copy(seen_b[:, :], seen[:, :]).then_inc(s_seen, 1)
                        c.wait()
                        c.step(dve.scalar_tensor_tensor(lg2[:, :, :], oh1[:, :, :], -3e38, lg[:, :, :], ALU.mult,
                                                        ALU.add))
                        aside(4)
                    c.wait()
                dve.tensor_tensor(both[:, :, :], oh1[:, :, :], oh2[:, :, :], ALU.add).then_inc(s_both, 1)

            def places(j, c, k, ids_of):
                dve.wait_ge(s_both, j + 1)
                c.step(dve.tensor_reduce(blk_sum[:, :], both[:, :, :].rearrange("p b e -> p e b"), AXX, ALU.add))
                dve.tensor_copy(meta[:, :, 1], pick[:, 0, :])
                c.wait()
                dve.tensor_tensor(seen[:, :], seen[:, :], blk_sum[:, :], ALU.add)
                dve.wait_ge(s_egap, j + 1)
                c.step(dve.tensor_scalar(den[:, :], egap[:, :], 1.0, None, ALU.add))
                dve.tensor_copy(meta[:, :, 0], ids[:, ids_of])
                c.wait()
                c.step(dve.reciprocal(den[:, :], den[:, :]))
                dve.wait_ge(s_rank_ps, j + 1)
                c.step(dve.tensor_tensor(rk[:, :, :], ps_r, spread(ecap[:, :], ALLE, 1), ALU.add))
                c.wait()
                c.step(dve.tensor_scalar(den[:, :], den[:, :], 1.0 / WS, None, ALU.mult))
                dve.tensor_tensor(eq[:, :, :], rk[:, :, :], oh1[:, :, :], ALU.mult)
                c.wait()
                c.step(dve.tensor_tensor(meta[:, :, 3], den[:, :], egap[:, :], ALU.mult))
                c.step(dve.tensor_tensor(lg2[:, :, :], rk[:, :, :], oh2[:, :, :], ALU.mult))
                c.wait()
                dve.tensor_tensor(meta[:, :, 2], den[:, :], meta[:, :, 3], ALU.subtract)
                dve.tensor_reduce(pos[:, 0, :], eq[:, :, :], AXX, ALU.add)
                dve.tensor_reduce(pos[:, 1, :], lg2[:, :, :], AXX, ALU.add).then_inc(s_pos, 1)

            def row_ends(k):
                dve.tensor_copy(row_out[:, k, :, D:ROW].bitcast(F32), meta[:, k * GB:(k + 1) * GB, :])

            def row_places(k):
                dve.tensor_copy(idx[:, k, :].rearrange("p (n b) -> p n b", n=2),
                                pos[:, :, k * GB:(k + 1) * GB]).then_inc(s_rows, 1)

            def logits(s, k, q):
                dve.wait_ge(s_l_ps, s - 1)
                dve.tensor_tensor(lg[:, (k + 2) % 4 * GB:((k + 2) % 4 + 1) * GB, :], ps_l,
                                  spread(unsc[:, q, :], [128, GB, E], 2), ALU.mult).then_inc(s_l, 1)

            def slot(s, k, j):
                q, q1 = k % 2, (k + 1) % 2
                roots = group(s + 3) or group(s - 1)
                v = veps[:, q1, :]
                if roots:
                    r = Chain(dve, s_root, (s + 3) * 9, 9)
                if group(s):
                    dve.wait_ge(s_p, s + 1)
                    dve.reciprocal(rsm[:, q, :], sm[:, q, :]).then_inc(s_rsm, 1)
                if group(s - 1):
                    dve.wait_ge(s_veps2, s)
                    dve.reciprocal(rec2[:, :], v[:, GB:2 * GB]).then_inc(s_rec2, 1)
                if group(s - 5) and k != 1:
                    row_ends((k + 3) % 4)
                if group(s - 1):
                    dve.wait_ge(s_rec2, s)
                    dve.tensor_tensor(v[:, 2 * GB:], rec2[:, :], mv2[:, q1, :, 1], ALU.mult).then_inc(s_vq, 1)
                if group(s - 5) and k != 1:
                    row_places((k + 3) % 4)
                if group(s - 1):
                    dve.wait_ge(s_vq, s)
                    dve.tensor_scalar(v[:, 2 * GB:], v[:, 2 * GB:], EPS, None, ALU.add).then_inc(s_vqe, 1)
                if group(s + 1):
                    dve.wait_ge(s_relu, s + 2)
                    if since(s, 1):
                        dve.wait_ge(s_pT_ps, s)
                    dve.tensor_tensor(p[:, q1, :, :], ps_s, e_sc[:, q1, :, :], ALU.add).then_inc(s_leaky, 1)
                if roots:
                    if group(s + 3):
                        dve.wait_ge(s_veps1, s + 4)
                    if group(s - 1):
                        dve.wait_ge(s_vqe, s)
                    r.step(dve.tensor_scalar(half_bits[:, :], v.bitcast(I32), 1, None, ALU.logical_shift_right))
                if group(s + 1):
                    dve.wait_ge(s_leaky, s + 2)
                    dve.tensor_reduce(nmx[:, q1, :], p[:, q1, :, :], AXX, ALU.max, negate=True).then_inc(s_nmx, 1)
                if roots:
                    r.wait()
                    r.step(dve.tensor_scalar(guess[:, :].bitcast(I32), half_bits[:, :], -1.0, GUESS, ALU.mult, ALU.add))
                if group(s):
                    dve.wait_ge(s_rsm, s + 1)
                    dve.wait_ge(s_att_ps, s + 1)
                    dve.tensor_tensor(hp[:, q, :, :], ps_att, spread(rsm[:, q, :], [128, GB, D], 2),
                                      ALU.mult).then_inc(s_hp, 1)
                if roots:
                    r.wait()
                    r.step(dve.tensor_tensor(root[:, :], guess[:, :], guess[:, :], ALU.mult))
                if group(s + 4):
                    dve.wait_ge(s_x_in, (s + 4 - q) * 8 + 16)
                    stats(s + 4, q, st1, s_stats1)
                if roots:
                    r.wait()
                    r.step(dve.scalar_tensor_tensor(root[:, :], root[:, :], -0.1875, v, ALU.mult, ALU.mult))
                g, kg = s - 3, (k + 1) % 4
                if group(g):
                    dve.wait_ge(s_xn, g + 1)
                    if since(g, 4):
                        dve.wait_ge(s_scat[kg], (g - kg) * 32)
                    hi, lo = (row_out[:, kg, :, n * D // 2:(n + 1) * D // 2].bitcast(F16) for n in range(2))
                    dve.tensor_copy(hi, xn[:, q1, :, :]).then_inc(s_xn_hi, 1)
                if roots:
                    r.wait()
                    r.step(dve.scalar_tensor_tensor(root[:, :], root[:, :], 0.5625, guess[:, :], ALU.add, ALU.mult))
                if group(g):
                    dve.wait_ge(s_xn_hi, g + 1)
                    dve.tensor_tensor(lo, xn[:, q1, :, :], hi, ALU.subtract).then_inc(s_xn_lo, 1)
                if roots:
                    r.wait()
                    r.step(dve.tensor_tensor(guess[:, :], root[:, :], root[:, :], ALU.mult))
                if group(s):
                    dve.wait_ge(s_ex, s + 1)
                    dve.scalar_tensor_tensor(x1[:, of(s), :], ex[:, q, :, :], 1.0, x1[:, of(s), :],
                                             ALU.min, ALU.add).then_inc(s_elu, 1)
                if roots:
                    r.wait()
                    r.step(dve.scalar_tensor_tensor(ratio[:, :], guess[:, :], 64 / 9, v, ALU.mult, ALU.mult))
                if group(s + 4):
                    mean_variance(s + 4, q, st1, mv1, s_stats1, s_aggr1)
                if roots:
                    r.wait()
                    r.step(dve.scalar_tensor_tensor(guess[:, :], ratio[:, :], -10 / 3, ratio[:, :], ALU.add, ALU.mult))
                if group(s):
                    dve.wait_ge(s_elu, s + 1)
                    dve.scalar_tensor_tensor(x1[:, of(s), :], hp[:, q, :, :], 0.0, x1[:, of(s), :],
                                             ALU.max, ALU.add).then_inc(s_x1, 1)
                if roots:
                    r.wait()
                    r.step(dve.scalar_tensor_tensor(rinv[:, q1, :], guess[:, :], 5.0, root[:, :], ALU.add, ALU.mult))
                if group(s + 4):
                    dve.wait_ge(s_aggr1, s + 5)
                    dve.tensor_scalar(veps[:, q, 0:GB], mv1[:, q, :, 1], EPS, None, ALU.add).then_inc(s_veps1, 1)
                if roots:
                    r.wait()
                    r.end()
                if group(s + 3):
                    dve.scalar_tensor_tensor(nbias1[:, q1, :], mv1[:, q1, :, 0], -1.0, rinv[:, q1, 0:GB],
                                             ALU.mult, ALU.mult).then_inc(s_nbias1, 1)
                if group(s - 1):
                    dve.tensor_tensor(rtot[:, q1, :], rinv[:, q1, GB:2 * GB], rinv[:, q1, 2 * GB:], ALU.mult).then_inc(s_rtot, 1)
                    dve.tensor_tensor(unsc[:, q1, :], veps[:, q1, 2 * GB:], rinv[:, q1, 2 * GB:], ALU.mult)
                if group(s) and not routes(s, k):
                    dve.wait_ge(s_x1, s + 1)
                    stats(s, q, st2, s_stats2)
                if group(s - 1):
                    dve.wait_ge(s_rtot, s)
                    dve.scalar_tensor_tensor(nbias2[:, q1, :], mv2[:, q1, :, 0], -1.0, rtot[:, q1, :],
                                             ALU.mult, ALU.mult).then_inc(s_scales, 1)
                if group(s) and not routes(s, k):
                    mean_variance(s, q, st2, mv2, s_stats2, s_aggr2)
                if isinstance(s, int) and 0 <= s + 3 < E:
                    e = s + 3
                    v = slice(e * H, (e + 1) * H)
                    dve.wait_ge(s_w_hi, 2 * e + 1)
                    dve.scalar_tensor_tensor(w1l[:, v], w_stage[:, e % 2 * 2, :], g_ws[:, e:e + 1], w1h[:, v],
                                             ALU.mult, ALU.subtract).then_inc(s_w_lo, 1)
                    dve.wait_ge(s_w_hi, 2 * e + 2)
                    dve.scalar_tensor_tensor(w2l[:, v], w_stage[:, e % 2 * 2 + 1, :], WS, w2h[:, v],
                                             ALU.mult, ALU.subtract).then_inc(s_w_lo, 1)
                    if e == E - 1:
                        dve.wait_ge(s_b1_mm, E)
                        dve.tensor_tensor(b1c[:, :], ps[:, 7, 0:E * HC], cols[:, 0:E * HC], ALU.add).then_inc(s_b1c, 1)
                if routes(s, k):
                    c = Chain(dve, s_route, j * ROUTE, ROUTE)
                    logits(s, k, q)

                    def stats_aside(n):
                        if group(s):
                            if n == 0:
                                dve.wait_ge(s_x1, s + 1)
                            if n == GB:
                                dve.wait_ge(s_stats2, s + 1)
                            dve.nop(nofuse=True)
                            b = n % GB
                            if n < GB:
                                ins = dve.bn_stats(st2[:, q, b, :], x1_of(s, b))
                            else:
                                ins = dve.bn_aggr(mv2[:, q, b, :], st2[:, q, b, :])
                            if n % GB == GB - 1:
                                ins.then_inc(s_stats2 if n < GB else s_aggr2, 1)
                    picks(j, c, stats_aside)
                if group(s):
                    dve.wait_ge(s_aggr2, s + 1)
                    dve.tensor_scalar(veps[:, q, GB:2 * GB], mv2[:, q, :, 1], EPS, None, ALU.add).then_inc(s_veps2, 1)
                if group(s - 2) and not routes(s, k):
                    logits(s, k, q)
                if routes(s, k):
                    places(j, c, k, bass.ds(j * BLK, BLK))
                    c.end()
                if group(s - 5) and k == 1:
                    dve.wait_ge(s_pos, j + 1)
                    row_ends((k + 3) % 4)
                    row_places((k + 3) % 4)
            phase_a(dve, slot)

            c = Chain(dve, s_tab_chain, 0, 33)
            c(dve.tensor_copy(seen_b[:, :], seen[:, :]))
            dve.wait_ge(s_cnt_ps, 1)
            dve.memset(t0[:, 0:1], 0.0)
            dve.tensor_copy(tabs[:, 2 * NT:], ps[0:1, 7, 0:E])
            c(dve.tensor_scalar(til_i[:, :], ps[:, 7, 0:E], TP - 1.0, None, ALU.add))
            c(dve.tensor_scalar(til_i[:, :], til_i[:, :], TP.bit_length() - 1, None, ALU.logical_shift_right))
            c(dve.tensor_copy(til[:, :], til_i[:, :]))
            c(dve.tensor_tensor_scan(t0[:, 1:], til[:, :], zero8[:, :], 0.0, ALU.add, ALU.add))
            c(dve.tensor_scalar(jump[:, :], til[:, :], -float(TP), float(CAP), ALU.mult, ALU.add))
            c(dve.memset(ef[:, :], 0.0))
            c(dve.tensor_scalar(rf[:, :], tile_no[:, :], float(TP), None, ALU.mult))
            for e in range(1, E):
                c(dve.tensor_scalar(past[:, :], tile_no[:, :], t0[:, e:e + 1], None, ALU.is_ge))
                c(dve.tensor_tensor(ef[:, :], ef[:, :], past[:, :], ALU.add))
                c(dve.scalar_tensor_tensor(rf[:, :], past[:, :], jump[:, e - 1:e], rf[:, :], ALU.mult, ALU.add))
            c(dve.tensor_scalar(past[:, :], tile_no[:, :], t0[:, E:E + 1], None, ALU.is_lt))
            c(dve.scalar_tensor_tensor(rf[:, :], rf[:, :], -float(E * CAP), past[:, :], ALU.add, ALU.mult))
            c(dve.tensor_scalar(tabs[:, 0:NT], rf[0:1, :], float(E * CAP), None, ALU.add))
            c(dve.tensor_scalar(code[:, :], ef[:, :], -1.0, float(E), ALU.mult, ALU.add))
            c.end()
            dve.tensor_copy(tabs[:, NT:2 * NT], ef[0:1, :]).then_inc(s_tab, 1)

            def slot_b(s, k):
                t, q, kr = s + 1, (k + 1) % 2, (k + 1) % RB
                if tile(t):
                    meta_in = row_in[:, kr, :, D:ROW].bitcast(F32)
                    dve.wait_ge(s_rT_ps, t + 1)
                    if since(t, RB):
                        dve.wait_ge(s_y_out[kr % YB], (t - kr) * (16 * TC // YB) + (kr // YB + 1 - RB // YB) * 16 * TC)
                    dve.nop(nofuse=True)
                    dve.tensor_scalar(is_first[:, :], meta_in[:, :, 1], code[:, bass.ds(t, 1)], None,
                                      ALU.is_equal).then_inc(s_sel, 1)
                    dve.wait_ge(s_sel, 3 * t + 1)
                    dve.tensor_tensor(y_idx[:, kr, :], meta_in[:, :, 0], is_first[:, :], ALU.subtract)
                    dve.tensor_tensor(w_sel[:, kr, :], meta_in[:, :, 2], is_first[:, :], ALU.mult).then_inc(s_sel, 1)
                    dve.wait_ge(s_sel, 3 * t + 2)
                    dve.tensor_tensor(w_sel[:, kr, :], w_sel[:, kr, :], meta_in[:, :, 3], ALU.add).then_inc(s_sel, 1)
                if tile(t):
                    if since(t, 2):
                        dve.wait_ge(s_down_ps, t - 1)
                    for half in range(2):
                        v = slice(half * HC // 2, (half + 1) * HC // 2)
                        dve.wait_ge(s_gelu, 2 * t + (half + 1))
                        dve.tensor_copy(hid_h(q)[:, v, :], hid(q)[:, v, :]).then_inc(s_hid_hi, 1)
                        dve.wait_ge(s_hid_hi, 2 * t + (half + 1))
                        dve.tensor_tensor(hid_l(q)[:, v, :], hid(q)[:, v, :], hid_h(q)[:, v, :],
                                          ALU.subtract).then_inc(s_hid_lo, 1)
            phase_b(dve, slot_b)

            with dve.Fori(0, B // CB // 2) as i:
                for q in range(2):
                    v = bass.ds(i * 2 * CB + q * CB, CB)
                    dve.wait_ge(s_y_in[q], i * 16 + 16)
                    dve.tensor_tensor(x1[:, v, :], x1[:, v, :], y_in(q)[:, :, 0:D], ALU.add).then_inc(s_c_half, 1)
                    dve.wait_ge(s_c_half, i * 2 + (q + 1))
                    dve.scalar_tensor_tensor(x1[:, v, :], x1[:, v, :], -1.0, y_in(q)[:, :, D:2 * D],
                                             ALU.add, ALU.add).then_inc(s_c_sum, 1)

        @block.tensor
        def _(pe):
            pe.wait_ge(s_const, 16)
            pe.wait_ge(s_w_rows, 16 * 9)
            pe.transpose(ps[:, 0, 0:50], small_rows[0:50, :], ident[0:50, 0:50]).then_inc(s_cols_T, 1)
            pe.transpose(ps[:, 1, 0:128], w_gnn[:, :], ident[:, :]).then_inc(s_wT_T, 1)
            pe.wait_ge(s_cols, 1)
            pe.wait_ge(s_wT, 1)
            pe.matmul(ps[:, 2, 0:2], w_gnnT[:, :], cols[:, 48:50], start=True, stop=True)
            pe.matmul(ps[:, 2, 2:2 + E], ones_row[:, :], br_row[:, :], start=True, stop=True).then_inc(s_wa_mm, 1)
            pe.wait_ge(s_reps, 1)

            def transposes(dst, src, q):
                for b in range(GB):
                    last = pe.transpose(dst[:, b, :], src[:, q, b, :], ident[:, :])
                return last

            def slot(s, k, j):
                if isinstance(s, int) and 0 <= s + 3 < E:
                    e = s + 3
                    pe.wait_ge(s_w_staged, 16 * (2 * e + 1))
                    for c in range(HC):
                        last = pe.matmul(ps[:, 7, e * HC + c:e * HC + c + 1], w_stage[:, e % 2 * 2, c * 128:(c + 1) * 128],
                                         cols[:, 40 + e:41 + e], start=True, stop=True)
                    last.then_inc(s_b1_mm, 1)
                g, q = s + 2, k % 2
                if group(g):
                    pe.wait_ge(s_hT, g + 1)
                    if since(g, 1):
                        pe.wait_ge(s_leaky, g)
                    pe.matmul(ps_s, ident_b[:, :], mask_b[:, :].unsqueeze(1).to_broadcast([128, GB, 128]),
                              start=True, stop=False)
                    pe.matmul(ps_s, wa2_rep[:, :], hT[:, q, :, :], start=False, stop=False)
                    for b in range(GB):
                        last = pe.matmul(ps_s[:, b, :], hT[:, q, b, :], wa1_rep[:, :], start=False, stop=b == GB - 1)
                    last.then_inc(s_s_ps, 1)
                g, q = s + 1, (k + 1) % 2
                if group(g):
                    pe.wait_ge(s_p, g + 1)
                    if since(g, 1):
                        pe.wait_ge(s_pT, g)
                    transposes(ps_pT, p, q).then_inc(s_pT_ps, 1)
                g, q = s - 2, k % 2
                if group(g):
                    pe.wait_ge(s_xT, g + 1)
                    if since(g, 1):
                        pe.wait_ge(s_l, g)
                    for b in range(GB):
                        last = pe.matmul(ps_l[:, b, :], xnT[:, q, b, :], wr[:, :], start=True, stop=True)
                    last.then_inc(s_l_ps, 1)
                g, q = s + 1, (k + 1) % 2
                if group(g):
                    pe.wait_ge(s_pT, g + 1)
                    pe.wait_ge(s_wh, g + 1)
                    if since(g, 1):
                        pe.wait_ge(s_hp, g)
                    for b in range(GB):
                        last = pe.matmul(ps_att[:, b, :], pT[:, q, b, :], wh[:, q, b, :], start=True, stop=True)
                    last.then_inc(s_att_ps, 1)
                g, q = s + 3, (k + 3) % 2
                if group(g):
                    pe.wait_ge(s_h, g + 1)
                    if since(g, 1):
                        pe.wait_ge(s_hT, g)
                    transposes(ps_hT, h, q).then_inc(s_hT_ps, 1)
                g, q = s - 1, (k - 1) % 2
                if group(g):
                    pe.wait_ge(s_xn, g + 1)
                    if since(g, 1):
                        pe.wait_ge(s_xT, g)
                    transposes(ps_xT, xn, q).then_inc(s_xT_ps, 1)
                g, q = s + 3, (k + 3) % 2
                if group(g):
                    pe.wait_ge(s_hT, g + 1)
                    if since(g, 1):
                        pe.wait_ge(s_wh, g)
                    for b in range(GB):
                        last = pe.matmul(ps_wh[:, b, :], hT[:, q, b, :], w_gnn[:, :], start=True, stop=True)
                    last.then_inc(s_wh_ps, 1)
                if routes(s, k):
                    pe.wait_ge(s_seen, j + 1)
                    pe.wait_ge(s_both, j + 1)
                    pe.wait_ge(s_b1c, 1)
                    if since(j, 1):
                        pe.wait_ge(s_route, j * ROUTE)
                    pe.matmul(ps_r, ones_b[:, :], seen_b[:, :].unsqueeze(1).to_broadcast([128, BLK, E]),
                              start=True, stop=False)
                    for b in range(BLK - 1):
                        pe.matmul(ps_r[:, b + 1:BLK, :], ones_b[:, :],
                                  both[:, b:b + 1, :].to_broadcast([128, BLK - 1 - b, E]),
                                  start=False, stop=False)
                    last = pe.matmul(ps_r, tri_b[:, :], both[:, :, :], start=False, stop=True)
                    last.then_inc(s_rank_ps, 1)
            phase_a(pe, slot)
            pe.wait_ge(s_tab_chain, 1)
            pe.matmul(ps[:, 7, 0:E], ones_b[:, :], seen_b[:, :], start=True, stop=True).then_inc(s_cnt_ps, 1)
            pe.wait_ge(s_b2_moved, 32)
            pe.wait_ge(s_tab, 1)

            expert_of = {}

            def expert(t, k):
                e = expert_of.get(k)
                if e is None:
                    e = pe.value_load(tabs[0:1, bass.ds(t + NT, 1)], min_val=0, max_val=E - 1)
                expert_of.clear()
                expert_of[k] = e
                return e

            def slot_b(s, k):
                t, q, kr = s + 2, k % 2, (k + 2) % RB
                if tile(t):
                    pe.wait_ge(s_rows_in[kr], (t - kr) * (16 // RB) + 16)
                    if since(t, 1):
                        pe.wait_ge(s_rT, t)
                    for part in range(2):
                        for c in range(TC):
                            last = pe.matmul(ps_rT[:, part, c * 128:(c + 1) * 128],
                                             row_in[:, kr, c, part * (D // 2):(part + 1) * (D // 2)].bitcast(F16),
                                             ident16[:, :], start=True, stop=True)
                    last.then_inc(s_rT_ps, 1)
                t, q = s + 1, (k + 1) % 2
                if tile(t):
                    e = expert(t, (k + 1) % RB)
                    pe.wait_ge(s_rT, t + 1)
                    if since(t, 1):
                        pe.wait_ge(s_gelu, 2 * t)
                    for c in range(HC):
                        v = bass.ds(e * H + c * 128, 128)
                        pe.matmul(ps_up[:, c, :], w1h[:, v], rT[:, q, 0:TP], start=True, stop=False)
                        pe.matmul(ps_up[:, c, :], w1h[:, v], rT[:, q, TP:], start=False, stop=False)
                        last = pe.matmul(ps_up[:, c, :], w1l[:, v], rT[:, q, 0:TP], start=False, stop=True)
                        if c % (HC // 2) == HC // 2 - 1:
                            last.then_inc(s_up_ps, 1)
                t, q = s, k % 2
                if tile(t):
                    e = expert(t, k)
                    pe.wait_ge(s_hid_lo, 2 * t + 2)
                    if since(t, 2):
                        pe.wait_ge(s_yw, t - 1)
                    pe.matmul(ps_y(q), ones2[:, :], b2_hl[:, bass.ds(e * D, D)].unsqueeze(1).to_broadcast([2, TC, D]),
                              start=True, stop=False)
                    for c in range(HC):
                        v = bass.ds(e * H + c * D, D)
                        for part, w in ((hid_h, w2h), (hid_l, w2h), (hid_h, w2l)):
                            for n in range(TC):
                                last = pe.matmul(ps_y(q)[:, n, :], part(q)[:, c, n * 128:(n + 1) * 128], w[:, v],
                                                 start=False, stop=c == HC - 1 and w is w2l and n == TC - 1)
                    last.then_inc(s_down_ps, 1)
            phase_b(pe, slot_b)


_INS = ['x', 'adj', 'L0_gnn_W', 'L0_gnn_a', 'L0_ffn_Wr', 'L0_ffn_br', 'L0_ffn_ln_g', 'L0_ffn_ln_b', 'L0_ffn_W1',
        'L0_ffn_b1', 'L0_ffn_W2', 'L0_ffn_b2']
_OUTS = [((B, N, D), 'float32')]


def kernel(**inputs):
    import numpy as _np
    import concourse.bacc as _bacc
    from concourse import mybir as _mybir
    from concourse.bass_utils import run_bass_kernel_spmd as _run

    nc = _bacc.Bacc("TRN2", target_bir_lowering=False, num_devices=1)
    arrays, args = {}, []
    for name in _INS:
        v = _np.ascontiguousarray(inputs[name])
        arrays[f"in_{name}_dram"] = v
        args.append(nc.dram_tensor(f"in_{name}_dram", v.shape, _mybir.dt.from_np(v.dtype), kind="ExternalInput").ap())
    for i, (shape, dtype) in enumerate(_OUTS):
        dt = _mybir.dt.from_np(_np.dtype(dtype))
        args.append(nc.dram_tensor(f"out_{i}_dram", shape, dt, kind="ExternalOutput").ap())
    program(nc, *args)
    r = _run(nc, [arrays], core_ids=[0])
    got = tuple(r.results[0][f"out_{i}_dram"] for i in range(len(_OUTS)))
    return got[0]
```
